# Optimizing a Trainium2 kernel written in Bass

```python
import numpy as np
import jax
import jax.numpy as jnp

def _softmax(x, axis=-1):
    return jax.nn.softmax(x, axis=axis)

def _gelu(x):
    return jax.nn.gelu(x, approximate=True)

def _silu(x):
    return jax.nn.silu(x)

def _sigmoid(x):
    return jax.nn.sigmoid(x)

def _layernorm(x, axis=-1, eps=1e-05):
    m = jnp.mean(x, axis=axis, keepdims=True)
    v = jnp.var(x, axis=axis, keepdims=True)
    return (x - m) / jnp.sqrt(v + eps)

def _scatter_add(tgt, idx, src, axis=0):
    return tgt.at[idx].add(src)

def _segment_sum(src, seg, n):
    return jax.ops.segment_sum(src, seg, n)
kernel_name = 'mk_adj_ffn_d1_adj_r2_ac410e'

def setup_inputs(seed: int=0):
    np.random.seed(seed)
    _w = jnp.asarray

    def _rec_inputs():
        import jax
        import jax.numpy as jnp
        _gk = jax.random.key(seed)
        x = 7.22e-05 + 1 * jax.random.normal(jax.random.fold_in(_gk, 1), (1354, 512), jnp.float32)
        _a = jax.random.bernoulli(jax.random.fold_in(_gk, 2), 0.00590842, (1354, 1354))
        _a = jnp.logical_or(_a, jnp.swapaxes(_a, -1, -2))
        _a = jnp.logical_or(_a, jnp.eye(1354, dtype=bool))
        _af = _a.astype(jnp.float32)
        _af = _af * jax.random.uniform(jax.random.fold_in(_gk, 3), (1354, 1354), jnp.float32, 0.05, 1)
        adj = _af
        return (x, adj)
    x, adj = _rec_inputs()

    def _L0_gnn_setup():
        import jax, jax.numpy as jnp
        import numpy as np
        N = 4096
        IN_FEATURES = 512
        OUT_FEATURES = 512
        key = jax.random.key(seed)
        k_x, k_adj, k_w, k_b = jax.random.split(key, 4)
        x = jax.random.normal(k_x, (N, IN_FEATURES), dtype=jnp.float32)
        adj = jax.random.uniform(k_adj, (N, N), dtype=jnp.float32)
        stdv = 1.0 / np.sqrt(OUT_FEATURES)
        weight = jax.random.uniform(k_w, (IN_FEATURES, OUT_FEATURES), dtype=jnp.float32, minval=-stdv, maxval=stdv)
        bias = jax.random.uniform(k_b, (OUT_FEATURES,), dtype=jnp.float32, minval=-stdv, maxval=stdv)
        return {'x': x, 'adj': adj, 'weight': weight, 'bias': bias}
    _L0_gnn_all = _L0_gnn_setup()
    _L0_gnn_in = {k: v for k, v in _L0_gnn_all.items() if k in ('weight', 'bias')}
    del _L0_gnn_all

    def _L0_ffn_setup():
        import jax, jax.numpy as jnp
        import numpy as np
        LOOPS = 2
        NUM_GROUPS = 4
        EXPERTS_PER_GROUP = 2
        NUM_EXPERTS = NUM_GROUPS * EXPERTS_PER_GROUP
        GROUPS_TOP_K = 2
        TOP_K = 1
        RMS_EPS = 1e-06
        EPS = 1e-09

        def _rmsnorm(x, w):
            return x * jax.lax.rsqrt(jnp.mean(x * x, axis=-1, keepdims=True) + RMS_EPS) * w

        def _combine_weights(x_flat, w_macro, w_micro):
            T = x_flat.shape[0]
            macro = jax.nn.softmax(x_flat @ w_macro.T, axis=-1)
            mvals, midx = jax.lax.top_k(macro, GROUPS_TOP_K)
            mvals = mvals / (jnp.sum(mvals, axis=-1, keepdims=True) + EPS)
            micro = jax.nn.softmax(jnp.einsum('td,ged->tge', x_flat, w_micro), axis=-1)
            uvals, uidx = jax.lax.top_k(micro, TOP_K)
            uvals = uvals / (jnp.sum(uvals, axis=-1, keepdims=True) + EPS)
            tok = jnp.arange(T)
            combine = jnp.zeros((T, NUM_EXPERTS), x_flat.dtype)
            for s in range(GROUPS_TOP_K):
                g = midx[:, s]
                wg = mvals[:, s:s + 1]
                li = uidx[tok, g]
                lv = uvals[tok, g]
                eidx = g[:, None] * EXPERTS_PER_GROUP + li
                combine = combine.at[tok[:, None], eidx].add(lv * wg)
            return combine
        key = jax.random.key(seed)
        ks = jax.random.split(key, 6)
        B, S, D, F = (2, 512, 512, 1024)
        return {'z': jax.random.normal(ks[0], (B, S, D), jnp.float32), 'norm_w': jnp.ones((D,), jnp.float32), 'w_macro': jax.random.normal(ks[1], (NUM_GROUPS, D), jnp.float32) * D ** (-0.5), 'w_micro': jax.random.normal(ks[2], (NUM_GROUPS, EXPERTS_PER_GROUP, D), jnp.float32) * D ** (-0.5), 'w1': jax.random.normal(ks[3], (NUM_EXPERTS, F, D), jnp.float32) * D ** (-0.5), 'w2': jax.random.normal(ks[4], (NUM_EXPERTS, D, F), jnp.float32) * F ** (-0.5)}
    _L0_ffn_all = _L0_ffn_setup()
    _L0_ffn_in = {k: v for k, v in _L0_ffn_all.items() if k in ('norm_w', 'w_macro', 'w_micro', 'w1', 'w2')}
    del _L0_ffn_all
    return {'x': x, 'adj': adj, 'L0_gnn_weight': _L0_gnn_in['weight'], 'L0_gnn_bias': _L0_gnn_in['bias'], 'L0_ffn_norm_w': _L0_ffn_in['norm_w'], 'L0_ffn_w_macro': _L0_ffn_in['w_macro'], 'L0_ffn_w_micro': _L0_ffn_in['w_micro'], 'L0_ffn_w1': _L0_ffn_in['w1'], 'L0_ffn_w2': _L0_ffn_in['w2']}

def reference(x, adj, L0_gnn_weight, L0_gnn_bias, L0_ffn_norm_w, L0_ffn_w_macro, L0_ffn_w_micro, L0_ffn_w1, L0_ffn_w2):
    import jax
    import jax.numpy as jnp

    def _L0_gnn_ref(x, adj, weight, bias):
        import jax, jax.numpy as jnp
        import numpy as np
        N = 4096
        IN_FEATURES = 512
        OUT_FEATURES = 512
        support = jnp.matmul(x, weight)
        output = jnp.matmul(adj, support)
        return output + bias

    def _L0_ffn_ref(z, norm_w, w_macro, w_micro, w1, w2):
        import jax, jax.numpy as jnp
        import numpy as np
        LOOPS = 2
        NUM_GROUPS = 4
        EXPERTS_PER_GROUP = 2
        NUM_EXPERTS = NUM_GROUPS * EXPERTS_PER_GROUP
        GROUPS_TOP_K = 2
        TOP_K = 1
        RMS_EPS = 1e-06
        EPS = 1e-09

        def _rmsnorm(x, w):
            return x * jax.lax.rsqrt(jnp.mean(x * x, axis=-1, keepdims=True) + RMS_EPS) * w

        def _combine_weights(x_flat, w_macro, w_micro):
            T = x_flat.shape[0]
            macro = jax.nn.softmax(x_flat @ w_macro.T, axis=-1)
            mvals, midx = jax.lax.top_k(macro, GROUPS_TOP_K)
            mvals = mvals / (jnp.sum(mvals, axis=-1, keepdims=True) + EPS)
            micro = jax.nn.softmax(jnp.einsum('td,ged->tge', x_flat, w_micro), axis=-1)
            uvals, uidx = jax.lax.top_k(micro, TOP_K)
            uvals = uvals / (jnp.sum(uvals, axis=-1, keepdims=True) + EPS)
            tok = jnp.arange(T)
            combine = jnp.zeros((T, NUM_EXPERTS), x_flat.dtype)
            for s in range(GROUPS_TOP_K):
                g = midx[:, s]
                wg = mvals[:, s:s + 1]
                li = uidx[tok, g]
                lv = uvals[tok, g]
                eidx = g[:, None] * EXPERTS_PER_GROUP + li
                combine = combine.at[tok[:, None], eidx].add(lv * wg)
            return combine
        B, S, D = z.shape
        T = B * S
        for _ in range(LOOPS):
            zn = _rmsnorm(z, norm_w)
            x = zn.reshape(T, D)
            combine = _combine_weights(x, w_macro, w_micro)
            h = jax.nn.silu(jnp.einsum('td,efd->tef', x, w1))
            y = jnp.einsum('tef,edf->ted', h, w2)
            mixed = jnp.einsum('ted,te->td', y, combine)
            z = z + mixed.reshape(B, S, D)
        return z
    x = x + _L0_gnn_ref(_layernorm(x, axis=-1), adj, L0_gnn_weight, L0_gnn_bias)
    x = x + _L0_ffn_ref(_layernorm(x, axis=-1)[None], L0_ffn_norm_w, L0_ffn_w_macro, L0_ffn_w_micro, L0_ffn_w1, L0_ffn_w2)[0]
    return x

_drawn_inputs = setup_inputs


def setup_inputs(seed=0):
    import zlib

    import numpy as np

    out = dict(_drawn_inputs(seed))
    spreads = {'L0_ffn_norm_w': (1.0, 0.2)}
    factors = {}
    for name, (base, spread) in spreads.items():
        noise = np.random.default_rng([zlib.crc32(name.encode()), seed]).standard_normal(out[name].shape)
        drawn = base * np.exp(spread * noise) if base else spread * noise
        out[name] = jnp.asarray(drawn.astype(out[name].dtype))
    for name, factor in factors.items():
        out[name] = (out[name] * factor).astype(out[name].dtype)
    return out
```

```python
from contextlib import ExitStack

import concourse.bass as bass
from concourse import mybir
from concourse.alu_op_type import AluOpType as ALU

ACT = mybir.ActivationFunctionType
AX = mybir.AxisListType
F32 = mybir.dt.float32
F32R = mybir.dt.float32r
BF16 = mybir.dt.bfloat16
I32 = mybir.dt.int32
U32 = mybir.dt.uint32

P = 128
LN_EPS = 1e-5
RMS_EPS = 1e-6
EPS = 1e-9
LOOPS = 2
HALF = 512


def adj_ffn_program(nc, x, adj_t, gnn_w, gnn_b, norm_w, w_route, w1, w2, out):
    N, D = out.shape
    n_tiles = x.shape[0] // P
    last_rows = N - (n_tiles - 1) * P
    E, _, _, F = w1.shape
    G = w_route.shape[2] - E
    PICK = E // G
    KD = D // P
    KF = F // P
    HALVES = F // HALF
    CHUNKS = 2 * KD
    CW = F
    REGION = (n_tiles + 1) * P
    ROW = D + 1 + E
    GT = 4
    groups = [list(range(a, min(a + GT, n_tiles))) for a in range(0, n_tiles, GT)]
    NQ = len(groups)
    ADJ = n_tiles * P
    FLAT = N * D // P
    PIECE = FLAT // 4
    N_LN = 2 * n_tiles

    with ExitStack() as ctx:
        def sb(name, shape, dt):
            return ctx.enter_context(nc.sbuf_tensor(name, shape, dt))

        def psum(name, shape):
            return ctx.enter_context(nc.psum_tensor(name, shape, F32))

        def sem(name):
            return ctx.enter_context(nc.semaphore(name))

        def dram(name, shape):
            return nc.dram_tensor(name, shape, F32, kind="Internal").ap()

        regions = dram("regions", (E * REGION, ROW))
        z_rows = dram("z_rows", (n_tiles * P + P, D))
        x1_rows = dram("x1_rows", (n_tiles * P, D))

        weights = sb("weights", [P, 2, 2, CHUNKS * CW], F32R)
        raw = sb("raw", [P, CHUNKS * CW], F32)
        even_area = weights[:, 0, :, :].rearrange("p a b -> p (a b)")
        odd_area = weights[:, 1, :, :].rearrange("p a b -> p (a b)")
        sup = [even_area[:, h * n_tiles * D:(h + 1) * n_tiles * D] for h in range(2)]
        gw0 = 2 * n_tiles * D
        gw = [even_area[:, gw0 + h * KD * D:gw0 + (h + 1) * KD * D] for h in range(2)]
        adj = [[odd_area[:, (2 * b + h) * ADJ:(2 * b + h + 1) * ADJ] for h in range(2)] for b in range(2)]
        adj_raw = [raw[:, b * ADJ:(b + 1) * ADJ] for b in range(2)]
        XR = 4
        x_raw = [raw[:, 2 * ADJ + b * D:2 * ADJ + (b + 1) * D] for b in range(XR)]
        gw_raw = raw[:, 2 * ADJ + XR * D:2 * ADJ + (XR + KD) * D]
        col0 = 2 * ADJ + (XR + KD) * D
        diff = raw[:, col0:col0 + P].bitcast(I32)
        tok_i = raw[:, col0 + P:col0 + P + n_tiles + 1].bitcast(I32)
        base_i = raw[:, col0 + 2 * P:col0 + 2 * P + E].bitcast(I32)

        zn = sb("zn", [P, 2, GT, ROW], F32)
        hidden = sb("hidden", [P, F], F32)
        xin = sb("xin", [P, ROW], F32)
        xT = [sb(f"xT_{h}", [P, KD * P], F32R) for h in ("hi", "lo")]
        hT = [sb(f"hT_{h}", [P, KF * P], F32R) for h in ("hi", "lo")]
        y_out = sb("y_out", [P, D], F32)
        y_row = sb("y_row", [P, 1], U32)
        zT = [y_out, sb("zT", [P, KD * P], F32)]
        w_norm = sb("w_norm", [P, D], F32)
        bias = xin[:, 0:D]
        ident = sb("ident", [P, P], F32)
        before = sb("before", [P, P], BF16)
        ones = sb("ones", [P, P], BF16)
        wr = sb("wr", [P, KD, G + E], F32)
        tok = sb("tok", [P, n_tiles + 1], F32)
        base0 = sb("base0", [P, E], F32)
        base = sb("base", [P, E], F32)
        valid = sb("valid", [P, 1], F32)
        lower = sb("lower", [P, G, G], F32)
        eps_ln = sb("eps_ln", [P, 1], F32)
        eps_rms = sb("eps_rms", [P, 1], F32)
        stats = sb("stats", [P, N_LN, 6], F32)
        mv = sb("mv", [P, N_LN, 2], F32)
        std = sb("std", [P, N_LN], F32)
        rstd = sb("rstd", [P, N_LN], F32)
        sumsq = sb("sumsq", [P, LOOPS * n_tiles], F32)
        rms = sb("rms", [P, LOOPS * n_tiles], F32)
        rrms = sb("rrms", [P, LOOPS * n_tiles], F32)
        lg = sb("lg", [P, GT, G + E], F32)
        gt_ = sb("gt", [P, GT, G, G], F32)
        eq_ = sb("eq", [P, GT, G, G], F32)
        rank = sb("rank", [P, GT, G], F32)
        pick = sb("pick", [P, GT, G, PICK], F32)
        chosen = [sb(f"chosen{s}", [P, GT, E], F32) for s in range(2)]
        mask = sb("mask", [P, GT + 1, E], BF16)
        top = sb("top", [P, GT], F32)
        d1 = sb("d1", [P, GT, G], F32)
        ex_in = sb("ex_in", [P, GT, 2 * G], F32)
        ex = sb("ex", [P, GT, 2 * G], F32)
        esum = sb("esum", [P, GT], F32)
        num = sb("num", [P, GT, G], F32)
        den = sb("den", [P, GT], F32)
        lv = sb("lv", [P, GT, G], F32)
        place = sb("place", [P, GT, E], F32)
        placed = [sb(f"placed{s}", [P, GT, E], F32) for s in range(2)]
        slot_f = sb("slot_f", [P, 2, GT], F32)
        slots = [sb(f"slots{b}", [P, 2, GT], U32) for b in range(2)]
        meta_next = sb("meta_next", [P, 1 + E], F32)
        meta_tile = sb("meta_tile", [P, 1 + E], F32)
        meta_y = sb("meta_y", [P, 2], F32)
        n_f = sb("n_f", [1, E], F32)
        n_i = sb("n_i", [1, E], I32)
        n_t = sb("n_t", [1, E], I32)
        pre = [sb(f"pre{k}", [1, 4 + E], F32) for k in range(4)]
        tiles_before = sb("tiles_before", [1, 1], F32)
        tile_table = [sb(f"tile_table{L}", [1, E + 1], I32) for L in range(LOOPS)]
        pad_table = [sb(f"pad_table{L}", [1, E], I32) for L in range(LOOPS)]

        h_ps = psum("h_ps", [P, 2, HALF])
        xt_ps = psum("xt_ps", [P, HALF])
        y_ps = psum("y_ps", [P, HALF])
        ht_ps = psum("ht_ps", [P, 2, HALF])
        lg_ps = psum("lg_ps", [P, HALF])
        rk_ps = psum("rk_ps", [P, HALF])
        turn_ps = [xt_ps, y_ps]
        rk = rk_ps[:, 0:(GT + 1) * E].rearrange("p (t e) -> p t e", e=E)

        s_gw = sem("gw_loaded")
        s_const = sem("const_loaded")
        s_x = [sem(f"x_loaded{b}") for b in range(XR)]
        s_adj = [sem(f"adj_loaded{b}") for b in range(2)]
        s_res = [sem(f"residual_loaded{b}") for b in range(2)]
        s_x1st = [sem(f"x1_stored{b}") for b in range(2)]
        s_zst = [sem(f"z_stored{b}") for b in range(2)]
        s_zin = [sem(f"z_loaded{b}") for b in range(2 * GT)]
        s_padz = sem("pad_rows_cleared")
        s_pad = sem("pads_filled")
        s_disp = [sem(f"dispatched{b}") for b in range(2)]
        s_xin = sem("xin_loaded")
        s_raw = [sem(f"chunk_loaded{c}") for c in range(CHUNKS)]
        s_added = sem("y_added")
        s_fx = sem("x1_reloaded")
        s_fz = [sem(f"z_reloaded{k}") for k in range(4)]
        s_out = sem("out_stored")
        s_iota = sem("iotas_made")
        s_made = sem("constants_made")
        s_step = sem("vector_steps")
        s_var = sem("variance_made")
        s_std = sem("std_made")
        s_xn = sem("xn_made")
        s_xnT = sem("xn_turned")
        s_xnh = sem("xn_hi_made")
        s_xnl = sem("xn_lo_made")
        s_gwh = sem("gw_hi_made")
        s_gwl = sem("gw_lo_made")
        s_sup = sem("support_summed")
        s_suph = sem("support_hi_made")
        s_supl = sem("support_lo_made")
        s_adjh = sem("adj_hi_made")
        s_adjl = sem("adj_lo_made")
        s_conv = sem("convolution_summed")
        s_x1 = sem("x1_made")
        s_z = sem("z_made")
        s_ss = sem("squares_summed")
        s_rms = sem("rms_made")
        s_zn = sem("zn_made")
        s_znT = sem("zn_turned")
        s_zT = sem("zT_copied")
        s_lg = sem("logits_made")
        s_lgt = sem("logits_taken")
        s_exi = sem("exponents_ready")
        s_exo = sem("exponentials_made")
        s_mask = sem("mask_made")
        s_rank = sem("ranks_made")
        s_slot = sem("slots_made")
        s_table = sem("tables_made")
        s_padt = sem("pad_tile_made")
        s_wh = sem("weight_hi_made")
        s_wl = sem("weight_lo_made")
        s_xt = sem("xin_turned")
        s_xh = sem("xT_hi_made")
        s_xl = sem("xT_lo_made")
        s_meta = sem("meta_taken")
        s_my = sem("meta_y_made")
        s_moved = sem("meta_moved")
        s_h = sem("hidden_half_summed")
        s_silu = sem("silu_half_made")
        s_ht = sem("hidden_half_turned")
        s_hh = sem("hT_hi_half_made")
        s_hl = sem("hT_lo_half_made")
        s_y = sem("y_summed")
        s_yt = sem("y_taken")
        s_begun = sem("y_adding")
        s_yf = sem("y_out_free")
        s_final = sem("final_added")


        def w1_part(par, h, kd, half):
            c0 = kd * CW + half * HALF
            return weights[:, par, h, c0:c0 + HALF]

        def w2_part(par, h, kf):
            c0 = KD * CW + kf * D
            return weights[:, par, h, c0:c0 + D]

        def chunk(h, par, c):
            return weights[:, par, h, c * CW:(c + 1) * CW]

        def raw_chunk(c):
            return raw[:, c * CW:(c + 1) * CW]

        def table_value(eng, L, e):
            cell = tile_table[L][0:1, e:e + 1] if isinstance(e, int) else tile_table[L][0:1, bass.ds(e, 1)]
            least = (e if isinstance(e, int) else 1) + E * L
            return eng.value_load(cell, min_val=least, max_val=4 * n_tiles * LOOPS)

        def experts(eng, L, tile):
            def one(e, par, start, prev):
                end = table_value(eng, L, e + 1)
                tile(start, e, par, True, prev, start)
                with eng.If(end > start + 1):
                    with eng.Fori(start + 1, end) as g:
                        tile(g, e, par, False, True, start)
                with eng.Else():
                    pass
                return end

            start = one(0, 0, table_value(eng, L, 0), False)
            with eng.Fori(1, E - 3, 2) as e:
                second = one(e, 1, table_value(eng, L, e), True)
                one(e + 1, 0, second, True)
            start = table_value(eng, L, E - 3)
            for e in range(E - 3, E):
                start = one(e, e % 2, start, True)
            return start

        def dispatched(b, below):
            return sum(2 * 16 * len(groups[q % NQ]) for q in range(below) if q % 2 == b)

        def z_loads(Q, t):
            return sum(q % 2 == Q % 2 and t < len(groups[q % NQ]) for q in range(NQ, Q + 1))

        def flat(rows):
            return rows.rearrange("r c -> (r c)").rearrange("(p f) -> p f", p=P)

        def z_flat(k):
            if k < 2:
                return raw[:, FLAT + k * PIECE:FLAT + (k + 1) * PIECE]
            return zn[:].rearrange("p a t c -> p (a t c)")[:, (k - 2) * PIECE:(k - 1) * PIECE]

        def rows_of(t):
            return last_rows if t == n_tiles - 1 else P

        block = ctx.enter_context(nc.Block())

        @block.sync
        def _(sp):
            def load_x(i):
                if i >= XR:
                    sp.wait_ge(s_xn, i - XR + 1)
                sp.dma_start(x_raw[i % XR], x[i * P:(i + 1) * P, :]).then_inc(s_x[i % XR], 16)

            def load_adj(i):
                if i >= 2:
                    sp.wait_ge(s_adjl, i - 1)
                sp.dma_start(adj_raw[i % 2], adj_t[i]).then_inc(s_adj[i % 2], 16)

            def load_residual(i):
                b = i % 2
                if i < 2:
                    sp.wait_ge(s_xnT, n_tiles)
                else:
                    sp.wait_ge(s_x1st[b], 16 * (i // 2))
                    sp.wait_ge(s_z, i - 1)
                sp.dma_start(hidden[:, b * D:(b + 1) * D], x[i * P:(i + 1) * P, :]).then_inc(s_res[b], 16)

            for i in range(XR):
                load_x(i)
                if i == 0:
                    sp.dma_start(gw_raw.rearrange("p (k n) -> p k n", k=KD),
                                 gnn_w.rearrange("(k p) n -> p k n", p=P)).then_inc(s_gw, 16)
            load_adj(0)
            load_adj(1)
            sp.dma_start(bias, gnn_b.partition_broadcast(P)).then_inc(s_const, 16)
            sp.dma_start(w_norm[:], norm_w.partition_broadcast(P)).then_inc(s_const, 16)
            sp.dma_start(wr[:], w_route.rearrange("k p n -> p k n")).then_inc(s_const, 16)
            for i in range(XR, n_tiles):
                load_x(i)
            load_residual(0)
            load_residual(1)
            for i in range(n_tiles):
                if i + 2 < n_tiles:
                    load_adj(i + 2)
                sp.wait_ge(s_x1, i + 1)
                sp.dma_start(x1_rows[i * P:(i + 1) * P, :], hidden[:, i % 2 * D:(i % 2 + 1) * D]
                             ).then_inc(s_x1st[i % 2], 16)
                sp.wait_ge(s_z, i + 1)
                sp.dma_start(z_rows[i * P:(i + 1) * P, :], zn[:, i // GT % 2, i % GT, 0:D]
                             ).then_inc(s_zst[i % 2], 16)
                if i + 2 < n_tiles:
                    load_residual(i + 2)

            for L in range(LOOPS):
                if L > 0:
                    sp.wait_ge(s_added, ended * 16)
                    for q, tiles in enumerate(groups):
                        Q = NQ * L + q
                        for t, i in enumerate(tiles):
                            if t == 0:
                                sp.wait_ge(s_disp[Q % 2], dispatched(Q % 2, Q))
                            sp.dma_start(zn[:, Q % 2, t, 0:D], z_rows[i * P:(i + 1) * P, :]
                                         ).then_inc(s_zin[Q % 2 * GT + t], 16)
                sp.wait_ge(s_padt, L + 1)
                if L == 0:
                    sp.dma_start(z_rows[n_tiles * P:, :], hidden[:, 0:D]).then_inc(s_padz, 16)
                sp.wait_ge(s_table, L + 1)
                for e in range(E):
                    first_pad = sp.value_load(pad_table[L][0:1, e:e + 1], min_val=0, max_val=(E - 1) * REGION + N)
                    sp.dma_start(regions[bass.ds(first_pad, P), :], hidden[:, 0:ROW]).then_inc(s_pad, 16)
                sp.wait_ge(s_pad, 16 * E * (L + 1))
                sp.wait_ge(s_padz, 16)
                for b in range(2):
                    sp.wait_ge(s_disp[b], dispatched(b, NQ * (L + 1)))

                def load_tile(g, e, par, first, prev, start):
                    if prev or L > 0:
                        sp.wait_ge(s_xt, g + L)
                        sp.wait_ge(s_meta, g + L)
                    row = e * REGION if first else e * REGION + (g - start) * P
                    if not isinstance(row, int):
                        row = nc.s_assert_within(row, 0, (E - 1) * REGION + ADJ, skip_runtime_bounds_check_because=
                                                 "g is one of the expert's tiles, of which there are at most n_tiles")
                    src = regions[row:row + P, :] if isinstance(row, int) else regions[bass.ds(row, P), :]
                    sp.dma_start(xin[:], src).then_inc(s_xin, 16)

                ended = experts(sp, L, load_tile)
                load_tile(ended, E - 1, 1, True, True, ended)

            sp.wait_ge(s_wl, LOOPS * E * CHUNKS)
            sp.dma_start(raw[:, 0:FLAT], flat(x1_rows[0:N, :])).then_inc(s_fx, 16)
            sp.wait_ge(s_added, ended * 16)
            for k in range(4):
                sp.dma_start(z_flat(k), flat(z_rows[0:N, :])[:, k * PIECE:(k + 1) * PIECE]).then_inc(s_fz[k], 16)
            for k in range(4):
                sp.wait_ge(s_final, k + 1)
                sp.dma_start(flat(out)[:, k * PIECE:(k + 1) * PIECE], raw[:, k * PIECE:(k + 1) * PIECE]
                             ).then_inc(s_out, 16)
            sp.wait_ge(s_x1st[0], 16 * ((n_tiles + 1) // 2))
            sp.wait_ge(s_x1st[1], 16 * (n_tiles // 2))
            sp.wait_ge(s_out, 64)

        @block.gpsimd
        def _(pool):
            pool.iota(diff, [[1, P]], base=0, channel_multiplier=-1)
            pool.iota(tok_i, [[P, n_tiles + 1]], base=0, channel_multiplier=1)
            pool.iota(base_i, [[REGION, E]], base=0, channel_multiplier=0).then_inc(s_iota, 1)
            for L in range(LOOPS):
                for q, tiles in enumerate(groups):
                    Q = NQ * L + q
                    pool.wait_ge(s_slot, Q + 1)
                    for t, i in enumerate(tiles):
                        n = rows_of(i)
                        for s in range(2):
                            pool.indirect_dma_start(
                                regions, bass.IndirectOffsetOnAxis(ap=slots[Q % 2][0:n, s, t:t + 1], axis=0),
                                zn[0:n, Q % 2, t, :], None).then_inc(s_disp[Q % 2], 16)
                if L == 0:
                    pool.wait_ge(s_padz, 16)
                    for b in range(2):
                        pool.wait_ge(s_zst[b], 16 * ((n_tiles + 1 - b) // 2))
                pool.wait_ge(s_table, L + 1)
                first_tile = table_value(pool, L, 0)
                ended = table_value(pool, L, E)
                with pool.Fori(first_tile, ended) as g:
                    pool.wait_ge(s_yt, g + 2)
                    pool.sem_inc(s_begun)
                    pool.indirect_dma_start(
                        z_rows, bass.IndirectOffsetOnAxis(ap=y_row[:, 0:1], axis=0),
                        y_out[:], None, compute_op=ALU.add).then_inc(s_added, 16)
                    pool.wait_ge(s_added, g * 16 + 16)
                    pool.nop().then_inc(s_yf, 1)

        @block.scalar
        def _(act):
            def split_hi(dst, src, ready):
                act.copy(dst, src).then_inc(ready, 1)

            def std_of(i):
                act.wait_ge(s_var, i + 1)
                act.activation(std[:, i:i + 1], mv[:, i, 1:2], ACT.Sqrt, bias=eps_ln[:, 0:1]).then_inc(s_std, 1)

            def adj_hi(i):
                act.wait_ge(s_adj[i % 2], 16 * (i // 2 + 1))
                if i >= 2:
                    act.wait_ge(s_conv, i - 1)
                split_hi(adj[i % 2][0], adj_raw[i % 2], s_adjh)

            def rms_of(n, buf, t):
                act.activation(ht_ps[:, 0, :], zn[:, buf, t, 0:D], ACT.Square,
                               accum_out=sumsq[:, n:n + 1]).then_inc(s_ss, 1)
                act.wait_ge(s_ss, n + 1)
                act.activation(rms[:, n:n + 1], sumsq[:, n:n + 1], ACT.Sqrt, scale=1.0 / D,
                               bias=eps_rms[:, 0:1]).then_inc(s_rms, 1)

            def copy_zT(n):
                act.wait_ge(s_znT, n + 1)
                if n >= 2:
                    act.wait_ge(s_lg, n - 1)
                act.copy(zT[n % 2][:], turn_ps[n % 2][:]).then_inc(s_zT, 1)

            def exps(Q, nt):
                act.wait_ge(s_exi, Q + 1)
                act.activation(ex[:, 0:nt, :], ex_in[:, 0:nt, :], ACT.Exp).then_inc(s_exo, 1)

            def load_chunk(en, c):
                w, k = (w1, c) if c < KD else (w2, c - KD)
                src = w[en, k] if isinstance(en, int) else w[bass.ds(en, 1), k, :, :].rearrange("a p n -> p (a n)")
                act.dma_start(raw_chunk(c), src).then_inc(s_raw[c], 16)

            act.wait_ge(s_gw, 16)
            split_hi(gw[0], gw_raw, s_gwh)
            act.wait_ge(s_made, 1)
            for i in range(n_tiles + 1):
                if i < n_tiles:
                    std_of(i)
                if i in (2, 4):
                    adj_hi(i // 2 - 1)
                if i >= 1:
                    j = i - 1
                    act.wait_ge(s_xnT, j + 1)
                    if j >= 2:
                        act.wait_ge(s_sup, j - 1)
                    split_hi(hT[0][:, j % 2 * D:(j % 2 + 1) * D], turn_ps[j % 2][:], s_xnh)
                    if j >= 1:
                        act.wait_ge(s_sup, j)
                        split_hi(sup[0][:, (j - 1) * D:j * D], h_ps[:, (j - 1) % 2, :], s_suph)
            act.wait_ge(s_sup, n_tiles)
            split_hi(sup[0][:, (n_tiles - 1) * D:], h_ps[:, (n_tiles - 1) % 2, :], s_suph)

            for i in range(n_tiles + 4):
                if i >= 1 and i + 1 < n_tiles:
                    adj_hi(i + 1)
                if i < n_tiles:
                    std_of(n_tiles + i)
                if i == n_tiles - 1:
                    act.wait_ge(s_adjl, n_tiles)
                    for c in range(CHUNKS):
                        load_chunk(0, c)
                if 2 <= i < n_tiles + 2:
                    copy_zT(i - 2)
                if i < n_tiles:
                    act.wait_ge(s_z, i + 1)
                    rms_of(i, i // GT % 2, i % GT)
                for q, tiles in enumerate(groups):
                    if i == tiles[-1] + 4:
                        exps(q, len(tiles))

            act.wait_ge(s_conv, n_tiles)
            for c in range(CHUNKS):
                act.wait_ge(s_raw[c], 16)
                split_hi(chunk(0, 0, c), raw_chunk(c), s_wh)
                act.wait_ge(s_wl, c + 1)
                load_chunk(1, c)

            for L in range(LOOPS):
                if L > 0:
                    for i in range(n_tiles + 4):
                        n = n_tiles * L + i
                        if 1 <= i < n_tiles + 1:
                            copy_zT(n - 1)
                        if i < n_tiles:
                            Q = NQ * L + i // GT
                            k = Q % 2 * GT + i % GT
                            act.wait_ge(s_zin[k], 16 * z_loads(Q, i % GT))
                            rms_of(n, Q % 2, i % GT)
                        for q, tiles in enumerate(groups):
                            if i == tiles[-1] + 4:
                                exps(NQ * L + q, len(tiles))

                act.wait_ge(s_table, L + 1)

                def x_hi(g):
                    act.wait_ge(s_xt, g + (L + 1))
                    split_hi(xT[0][:], xt_ps[:], s_xh)

                def tile(g, e, par, first, prev, start):
                    more = first and not (L == LOOPS - 1 and isinstance(e, int) and e == E - 1)
                    load = first and not (L == LOOPS - 1 and isinstance(e, int) and e >= E - 2)
                    en = e + E * L

                    def next_hi(c):
                        act.wait_ge(s_raw[c], 16 * (en + 2) if isinstance(en, int) else en * 16 + 32)
                        if prev or L > 0:
                            if c < KD:
                                act.wait_ge(s_h, start * HALVES)
                            else:
                                act.wait_ge(s_y, start)
                        split_hi(chunk(0, 1 - par, c), raw_chunk(c), s_wh)

                    if more:
                        next_hi(0)
                        next_hi(1)
                    for half in range(HALVES):
                        act.wait_ge(s_h, g * HALVES + (half + 1))
                        act.activation(hidden[:, half * HALF:(half + 1) * HALF], h_ps[:, half, :],
                                       ACT.Silu).then_inc(s_silu, 1)
                        if more and half == 0:
                            next_hi(2)
                    x_hi(g + 1)
                    if more:
                        next_hi(3)
                    if load:
                        for c in range(KD):
                            act.wait_ge(s_wl, en * CHUNKS + (CHUNKS + c + 1))
                            load_chunk((e + 2) % E if isinstance(e, int) else e + 2, c)
                    for half in range(HALVES):
                        act.wait_ge(s_ht, g * HALVES + (half + 1))
                        split_hi(hT[0][:, half * HALF:(half + 1) * HALF], ht_ps[:, half, :], s_hh)
                    if more:
                        for c in range(KD, CHUNKS):
                            next_hi(c)
                    if load:
                        for c in range(KD, CHUNKS):
                            act.wait_ge(s_wl, en * CHUNKS + (CHUNKS + c + 1))
                            load_chunk((e + 2) % E if isinstance(e, int) else e + 2, c)

                x_hi(table_value(act, L, 0))
                experts(act, L, tile)

        @block.tensor
        def _(pe):
            def turn(dst, src, kd0, n, ready):
                for k in range(n):
                    m = pe.transpose(dst[:, k * P:(k + 1) * P], src[:, (kd0 + k) * P:(kd0 + k + 1) * P], ident[:])
                m.then_inc(ready, 1)

            def product(dst, pairs, ready):
                for k, ((ah, al), (bh, bl)) in enumerate(pairs):
                    pe.matmul(dst, ah, bh, start=(k == 0), stop=False)
                    pe.matmul(dst, ah, bl, start=False, stop=False)
                    m = pe.matmul(dst, al, bh, start=False, stop=(k == len(pairs) - 1))
                m.then_inc(ready, 1)

            def turn_zn(n, buf, t):
                pe.wait_ge(s_zn, n + 1)
                if n >= 2:
                    pe.wait_ge(s_zT, n - 1)
                turn(turn_ps[n % 2], zn[:, buf, t, :], 0, KD, s_znT)

            def logits(n, Q, t):
                pe.wait_ge(s_zT, n + 1)
                if t == 0 and Q > 0:
                    pe.wait_ge(s_lgt, Q)
                c0 = t * (G + E)
                for k in range(KD):
                    m = pe.matmul(lg_ps[:, c0:c0 + G + E], zT[n % 2][:, k * P:(k + 1) * P], wr[:, k, :],
                                  start=(k == 0), stop=(k == KD - 1))
                m.then_inc(s_lg, 1)

            def ranks(Q, nt):
                pe.wait_ge(s_mask, Q + 1)
                pe.matmul(rk_ps[:, 0:(nt + 1) * E], before[:], mask[:, 0:nt + 1, :].rearrange("p t e -> p (t e)"),
                          start=True, stop=True)
                for t in range(nt):
                    m = pe.matmul(rk[:, t + 1:nt + 1, :], ones[:],
                                  mask[:, t:t + 1, :].broadcast_to([P, nt - t, E]),
                                  start=False, stop=True, skip_group_check=True)
                m.then_inc(s_rank, 1)

            pe.wait_ge(s_made, 1)
            for i in range(n_tiles + 1):
                if i < n_tiles:
                    pe.wait_ge(s_xn, i + 1)
                    if i >= 2:
                        pe.wait_ge(s_xnl, i - 1)
                    turn(turn_ps[i % 2], hidden[:, i % 2 * D:(i % 2 + 1) * D], 0, KD, s_xnT)
                if i >= 1:
                    j = i - 1
                    if j == 0:
                        pe.wait_ge(s_gwl, 1)
                    pe.wait_ge(s_xnl, j + 1)
                    if j >= 2:
                        pe.wait_ge(s_supl, j - 1)
                    c0 = j % 2 * D
                    product(h_ps[:, j % 2, :],
                            [([hT[h][:, c0 + k * P:c0 + (k + 1) * P] for h in range(2)],
                              [gw[h][:, k * D:(k + 1) * D] for h in range(2)]) for k in range(KD)], s_sup)
            pe.wait_ge(s_supl, n_tiles)
            for i in range(n_tiles + 4):
                if i < n_tiles:
                    pe.wait_ge(s_adjl, i + 1)
                    if i >= 2:
                        pe.wait_ge(s_x1, i - 1)
                    product(h_ps[:, i % 2, :],
                            [([adj[i % 2][h][:, j * P:(j + 1) * P] for h in range(2)],
                              [sup[h][:, j * D:(j + 1) * D] for h in range(2)]) for j in range(n_tiles)], s_conv)
                if 2 <= i < n_tiles + 2:
                    logits(i - 2, (i - 2) // GT, (i - 2) % GT)
                if 1 <= i < n_tiles + 1:
                    turn_zn(i - 1, (i - 1) // GT % 2, (i - 1) % GT)
                for q, tiles in enumerate(groups):
                    if i == tiles[-1] + 4:
                        ranks(q, len(tiles))

            for L in range(LOOPS):
                if L > 0:
                    for i in range(n_tiles + 4):
                        n = n_tiles * L + i
                        if i < n_tiles:
                            turn_zn(n, (NQ * L + i // GT) % 2, i % GT)
                        if 1 <= i < n_tiles + 1:
                            logits(n - 1, NQ * L + (i - 1) // GT, (i - 1) % GT)
                        for q, tiles in enumerate(groups):
                            if i == tiles[-1] + 4:
                                ranks(NQ * L + q, len(tiles))
                pe.wait_ge(s_table, L + 1)

                def turn_x(g):
                    pe.wait_ge(s_xin, g * 16 + 16 * (L + 1))
                    turn(xt_ps, xin, 0, KD, s_xt)

                def y_product(nxt, par, chunks):
                    pe.wait_ge(s_wl, chunks)
                    pe.wait_ge(s_yt, nxt)
                    for half in range(HALVES):
                        pe.wait_ge(s_hl, nxt * HALVES + (half + 1))
                        for kf in range(half * KF // HALVES, (half + 1) * KF // HALVES):
                            ah, al = (hT[h][:, kf * P:(kf + 1) * P] for h in range(2))
                            pe.matmul(y_ps[:], ah, w2_part(par, 0, kf), start=(kf == 0), stop=False)
                            pe.matmul(y_ps[:], ah, w2_part(par, 1, kf), start=False, stop=False)
                            m = pe.matmul(y_ps[:], al, w2_part(par, 0, kf), start=False, stop=(kf == KF - 1))
                    m.then_inc(s_y, 1)

                def tile(g, e, par, first, prev, start):
                    en = e + E * L
                    if first:
                        pe.wait_ge(s_wl, en * CHUNKS + KD)
                    pe.wait_ge(s_xl, g + (L + 1))
                    for half in range(HALVES):
                        product(h_ps[:, half, :],
                                [([xT[h][:, k * P:(k + 1) * P] for h in range(2)],
                                  [w1_part(par, h, k, half) for h in range(2)]) for k in range(KD)], s_h)
                    turn_x(g + 1)
                    if prev:
                        y_product(g, 1 - par if first else par, en * CHUNKS + (0 if first else CHUNKS))
                    for half in range(HALVES):
                        pe.wait_ge(s_silu, g * HALVES + (half + 1))
                        turn(ht_ps[:, half, :], hidden, half * KD, KD, s_ht)

                turn_x(table_value(pe, L, 0))
                ended = experts(pe, L, tile)
                y_product(ended, (E - 1) % 2, E * (L + 1) * CHUNKS)

        @block.vector
        def _(dve):
            steps = [0]

            def step(ins):
                steps[0] += 1
                ins.then_inc(s_step, 1)
                dve.wait_ge(s_step, steps[0])

            def lo(dst, src, hi, ready):
                dve.tensor_tensor(dst, src, hi.bitcast(F32), ALU.subtract).then_inc(ready, 1)

            def moments(i, src):
                step(dve.bn_stats(stats[:, i, :], src))
                dve.bn_aggr(mv[:, i, :], stats[:, i, :]).then_inc(s_var, 1)

            def normalise(i, dst, src, ready):
                dve.wait_ge(s_std, i + 1)
                step(dve.reciprocal(rstd[:, i:i + 1], std[:, i:i + 1]))
                dve.tensor_scalar(dst, src, mv[:, i, 0:1], rstd[:, i:i + 1], ALU.subtract,
                                  ALU.mult).then_inc(ready, 1)

            def adj_lo(i):
                dve.wait_ge(s_adjh, i + 1)
                lo(adj[i % 2][1], adj_raw[i % 2], adj[i % 2][0], s_adjl)

            def make_zn(n, buf, t):
                dve.wait_ge(s_rms, n + 1)
                step(dve.reciprocal(rrms[:, n:n + 1], rms[:, n:n + 1]))
                z = zn[:, buf, t, 0:D]
                dve.scalar_tensor_tensor(out=z, in0=z, scalar=rrms[:, n:n + 1], in1=w_norm[:], op0=ALU.mult,
                                         op1=ALU.mult).then_inc(s_zn, 1)

            def bc(ap, shape):
                return ap.broadcast_to(shape)

            def route_a(Q, tiles):
                nt = len(tiles)
                buf = Q % 2
                t_ = slice(0, nt)
                dve.wait_ge(s_lg, n_tiles * (Q // NQ) + tiles[-1] + 1)
                dve.tensor_copy(lg[:, t_, :].rearrange("p t e -> p (t e)"), lg_ps[:, 0:nt * (G + E)]
                                ).then_inc(s_lgt, 1)
                dve.wait_ge(s_lgt, Q + 1)
                macro = lg[:, t_, 0:G]
                u = lg[:, t_, G:].rearrange("p t (g k) -> p t g k", k=PICK)
                step(dve.tensor_reduce(top[:, t_], macro, AX.X, ALU.max))
                step(dve.tensor_tensor(d1[:, t_, :], u[:, :, :, 0], u[:, :, :, 1], ALU.subtract))
                dve.tensor_tensor(ex_in[:, t_, 0:G], macro, bc(top[:, t_].unsqueeze(2), [P, nt, G]), ALU.subtract)
                dve.scalar_tensor_tensor(out=ex_in[:, t_, G:], in0=d1[:, t_, :], scalar=-1.0, in1=d1[:, t_, :],
                                         op0=ALU.mult, op1=ALU.min).then_inc(s_exi, 1)
                for t in range(nt):
                    other = bc(lg[:, t, 0:G].unsqueeze(1), [P, G, G])
                    own = bc(lg[:, t, 0:G].unsqueeze(2), [P, G, G])
                    dve.tensor_tensor(gt_[:, t, :, :], other, own, ALU.is_gt)
                    ins = dve.tensor_tensor(eq_[:, t, :, :], other, own, ALU.is_equal)
                step(ins)
                flat_g = lambda a: a[:, t_, :, :].rearrange("p t g k -> p t (g k)")
                low = bc(lower[:].rearrange("p g k -> p (g k)").unsqueeze(1), [P, nt, G * G])
                step(dve.tensor_tensor(flat_g(eq_), flat_g(eq_), low, ALU.mult))
                step(dve.tensor_tensor(flat_g(gt_), flat_g(gt_), flat_g(eq_), ALU.add))
                step(dve.tensor_reduce(rank[:, t_, :], gt_[:, t_, :, :], AX.X, ALU.add))
                dve.tensor_tensor(pick[:, t_, :, 0], u[:, :, :, 0], u[:, :, :, 1], ALU.is_ge)
                step(dve.tensor_tensor(pick[:, t_, :, 1], u[:, :, :, 0], u[:, :, :, 1], ALU.is_lt))
                for s in range(2):
                    ins = dve.scalar_tensor_tensor(
                        out=chosen[s][:, t_, :].rearrange("p t (g k) -> p (t g) k", k=PICK),
                        in0=bc(rank[:, t_, :].rearrange("p t g -> p (t g)").unsqueeze(2), [P, nt * G, PICK]),
                        scalar=float(s), in1=pick[:, t_, :, :].rearrange("p t g k -> p (t g) k"),
                        op0=ALU.is_equal, op1=ALU.mult)
                step(ins)
                dve.memset(mask[:, nt, :], 0.0)
                full = nt - 1 if tiles[-1] == n_tiles - 1 else nt
                ins = dve.tensor_tensor(mask[:, 0:full, :], chosen[0][:, 0:full, :], chosen[1][:, 0:full, :], ALU.add)
                if full < nt:
                    step(dve.tensor_tensor(placed[0][:, full, :], chosen[0][:, full, :], chosen[1][:, full, :],
                                           ALU.add))
                    ins = dve.tensor_scalar(mask[:, full, :], placed[0][:, full, :], valid[:, 0:1], None, ALU.mult)
                ins.then_inc(s_mask, 1)

            def route_b(Q, tiles):
                nt = len(tiles)
                buf = Q % 2
                t_ = slice(0, nt)
                dve.wait_ge(s_exo, Q + 1)
                step(dve.tensor_reduce(esum[:, t_], ex[:, t_, 0:G], AX.X, ALU.add))
                step(dve.scalar_tensor_tensor(out=num[:, t_, :], in0=rank[:, t_, :], scalar=2.0, in1=ex[:, t_, 0:G],
                                              op0=ALU.is_lt, op1=ALU.mult))
                step(dve.tensor_reduce(den[:, t_], num[:, t_, :], AX.X, ALU.add))
                step(dve.scalar_tensor_tensor(out=den[:, t_], in0=esum[:, t_], scalar=EPS, in1=den[:, t_],
                                              op0=ALU.mult, op1=ALU.add))
                step(dve.reciprocal(den[:, t_], den[:, t_]))
                step(dve.tensor_scalar(lv[:, t_, :], ex[:, t_, G:], EPS, 1.0 + EPS, ALU.mult, ALU.add))
                step(dve.reciprocal(lv[:, t_, :], lv[:, t_, :]))
                step(dve.tensor_tensor(num[:, t_, :], num[:, t_, :], bc(den[:, t_].unsqueeze(2), [P, nt, G]),
                                       ALU.mult))
                step(dve.tensor_tensor(num[:, t_, :], num[:, t_, :], lv[:, t_, :], ALU.mult))
                for t, i in enumerate(tiles):
                    dve.tensor_tensor(zn[:, buf, t, D + 1:].rearrange("p (g k) -> p g k", k=PICK),
                                      bc(num[:, t, :].unsqueeze(2), [P, G, PICK]), pick[:, t, :, :], ALU.mult)
                dve.tensor_copy(zn[:, buf, t_, D:D + 1].rearrange("p t a -> p (t a)"), tok[:, tiles[0]:tiles[-1] + 1])
                dve.wait_ge(s_rank, Q + 1)
                step(dve.tensor_tensor(place[:, t_, :], rk[:, t_, :], bc(base[:].unsqueeze(1), [P, nt, E]), ALU.add))
                for s in range(2):
                    ins = dve.tensor_tensor(placed[s][:, t_, :], place[:, t_, :], chosen[s][:, t_, :], ALU.mult)
                step(ins)
                for s in range(2):
                    ins = dve.tensor_reduce(slot_f[:, s, t_], placed[s][:, t_, :], AX.X, ALU.add)
                step(ins)
                step(dve.tensor_tensor(base[:], base[:], rk[:, nt, :], ALU.add))
                dve.tensor_copy(slots[buf][:, :, t_], slot_f[:, :, t_]).then_inc(s_slot, 1)

            def tables(L):
                step(dve.tensor_copy(pad_table[L][:], base[0:1, :]))
                step(dve.tensor_tensor(n_f[:], base[0:1, :], base0[0:1, :], ALU.subtract))
                step(dve.tensor_scalar(n_i[:], n_f[:], float(P - 1), None, ALU.add))
                step(dve.tensor_scalar(n_t[:], n_i[:], P.bit_length() - 1, None, ALU.logical_shift_right))
                step(dve.tensor_scalar(pre[0][:, 4:], n_t[:], 1.0, None, ALU.max))
                for k in range(3):
                    step(dve.tensor_tensor(pre[k + 1][:, 4:], pre[k][:, 4:], pre[k][:, 4 - 2 ** k:4 + E - 2 ** k],
                                           ALU.add))
                dve.tensor_copy(tile_table[L][:, 0:1], tiles_before[:])
                step(dve.tensor_scalar(tile_table[L][:, 1:], pre[3][:, 4:], tiles_before[:, 0:1], None, ALU.add))
                dve.tensor_tensor(tiles_before[:], tiles_before[:], pre[3][:, 3 + E:], ALU.add).then_inc(s_table, 1)

            def pad_tile(L):
                step(dve.memset(hidden[:, 0:ROW], 0.0))
                dve.tensor_copy(hidden[:, D:D + 1], tok[:, n_tiles:n_tiles + 1]).then_inc(s_padt, 1)

            dve.memset(ones[:], 1.0)
            dve.memset(eps_ln[:], LN_EPS)
            dve.memset(eps_rms[:], RMS_EPS)
            for k in range(4):
                dve.memset(pre[k][:, 0:4], 0.0)
            dve.memset(tiles_before[:], 0.0)
            dve.memset(lower[:], 0.0)
            step(dve.memset(valid[:], 0.0))
            for g in range(1, G):
                dve.memset(lower[:, g, 0:g], 1.0)
            dve.memset(valid[0:last_rows, :], 1.0)
            dve.wait_ge(s_iota, 1)
            dve.tensor_scalar(ident[:], diff, 0.0, None, ALU.is_equal)
            dve.tensor_scalar(before[:], diff, 0.0, None, ALU.is_gt)
            dve.tensor_copy(tok[:], tok_i)
            dve.tensor_copy(base0[:], base_i)
            dve.tensor_copy(base[:], base_i).then_inc(s_made, 1)
            dve.nop().then_inc(s_yt, 1)
            dve.nop().then_inc(s_yf, 1)
            dve.nop().then_inc(s_hl, HALVES)

            for i in range(n_tiles + 1):
                if i < n_tiles:
                    dve.wait_ge(s_x[i % XR], 16 * (i // XR + 1))
                    moments(i, x_raw[i % XR])
                if i == 0:
                    dve.wait_ge(s_gwh, 1)
                    lo(gw[1], gw_raw, gw[0], s_gwl)
                if i < n_tiles:
                    if i >= 2:
                        dve.wait_ge(s_xnT, i - 1)
                    normalise(i, hidden[:, i % 2 * D:(i % 2 + 1) * D], x_raw[i % XR], s_xn)
                if i >= 1:
                    j = i - 1
                    c = slice(j % 2 * D, (j % 2 + 1) * D)
                    dve.wait_ge(s_xnh, j + 1)
                    lo(hT[1][:, c], turn_ps[j % 2][:], hT[0][:, c], s_xnl)
                    if j >= 1:
                        c = slice((j - 1) * D, j * D)
                        dve.wait_ge(s_suph, j)
                        lo(sup[1][:, c], h_ps[:, (j - 1) % 2, :], sup[0][:, c], s_supl)
                if i in (3, 5):
                    adj_lo((i - 3) // 2)
            c = slice((n_tiles - 1) * D, n_tiles * D)
            dve.wait_ge(s_suph, n_tiles)
            lo(sup[1][:, c], h_ps[:, (n_tiles - 1) % 2, :], sup[0][:, c], s_supl)

            dve.wait_ge(s_const, 48)
            for i in range(n_tiles + 4):
                if 1 <= i < n_tiles + 1:
                    j = i - 1
                    dve.wait_ge(s_zst[j % 2], 16 * (j // 2 + 1))
                    make_zn(j, j // GT % 2, j % GT)
                if i < n_tiles:
                    half = hidden[:, i % 2 * D:(i % 2 + 1) * D]
                    dve.wait_ge(s_conv, i + 1)
                    dve.wait_ge(s_res[i % 2], 16 * (i // 2 + 1))
                    step(dve.tensor_tensor(half, h_ps[:, i % 2, :], half, ALU.add))
                    dve.tensor_tensor(half, half, bias, ALU.add).then_inc(s_x1, 1)
                    dve.wait_ge(s_x1, i + 1)
                    moments(n_tiles + i, half)
                if i >= 1 and i + 1 < n_tiles:
                    adj_lo(i + 1)
                if i < n_tiles:
                    Q = i // GT
                    if Q >= 2 and i % GT == 0:
                        dve.wait_ge(s_disp[Q % 2], dispatched(Q % 2, Q))
                    normalise(n_tiles + i, zn[:, Q % 2, i % GT, 0:D], half, s_z)
                for q, tiles in enumerate(groups):
                    if i == tiles[-1] + 3:
                        route_a(q, tiles)
                    if i == tiles[-1] + 4:
                        route_b(q, tiles)

            def weight_lo(par, c, en):
                dve.wait_ge(s_wh, en * CHUNKS + (c + 1))
                lo(chunk(1, par, c), raw_chunk(c), chunk(0, par, c), s_wl)

            for L in range(LOOPS):
                if L > 0:
                    step(dve.tensor_copy(base[:], base0[:]))
                    for i in range(n_tiles + 4):
                        n = n_tiles * L + i
                        if i < n_tiles:
                            make_zn(n, (NQ * L + i // GT) % 2, i % GT)
                        for q, tiles in enumerate(groups):
                            if i == tiles[-1] + 3:
                                route_a(NQ * L + q, tiles)
                            if i == tiles[-1] + 4:
                                route_b(NQ * L + q, tiles)
                tables(L)
                dve.wait_ge(s_table, L + 1)
                if L == 0:
                    for b in range(2):
                        dve.wait_ge(s_x1st[b], 16 * ((n_tiles + 1 - b) // 2))
                pad_tile(L)
                if L == 0:
                    for c in range(CHUNKS):
                        weight_lo(0, c, 0)

                def x_lo(g):
                    dve.wait_ge(s_xh, g + (L + 1))
                    lo(xT[1][:], xt_ps[:], xT[0][:], s_xl)
                    if L > 0 or g is not first_tile:
                        dve.wait_ge(s_moved, g + L)
                    dve.tensor_copy(meta_next[:], xin[:, D:]).then_inc(s_meta, 1)

                def take_y(nxt):
                    dve.wait_ge(s_y, nxt)
                    dve.wait_ge(s_yf, nxt)
                    dve.tensor_copy(y_row[:], meta_y[:, 0:1])
                    dve.tensor_scalar(y_out[:], y_ps[:], meta_y[:, 1:2], None, ALU.mult).then_inc(s_yt, 1)

                def tile(g, e, par, first, prev, start):
                    more = first and not (L == LOOPS - 1 and isinstance(e, int) and e == E - 1)
                    en = e + E * L + 1
                    if more:
                        for c in range(3):
                            weight_lo(1 - par, c, en)
                    x_lo(g + 1)
                    if more:
                        weight_lo(1 - par, 3, en)
                    if prev:
                        take_y(g)
                    dve.wait_ge(s_yt, g + 1)
                    dve.wait_ge(s_moved, g + (L + 1))
                    dve.tensor_copy(meta_y[:, 0:1], meta_tile[:, 0:1])
                    w_col = meta_tile[:, 1 + e:2 + e] if isinstance(e, int) else meta_tile[:, bass.ds(e + 1, 1)]
                    dve.tensor_copy(meta_y[:, 1:2], w_col).then_inc(s_my, 1)
                    dve.wait_ge(s_my, g + 1)
                    dve.wait_ge(s_meta, g + (L + 2))
                    dve.tensor_copy(meta_tile[:], meta_next[:]).then_inc(s_moved, 1)
                    for half in range(HALVES):
                        c = slice(half * HALF, (half + 1) * HALF)
                        dve.wait_ge(s_hh, g * HALVES + (half + 1))
                        lo(hT[1][:, c], ht_ps[:, half, :], hT[0][:, c], s_hl)
                    if more:
                        for c in range(KD, CHUNKS):
                            weight_lo(1 - par, c, en)

                first_tile = table_value(dve, L, 0)
                x_lo(first_tile)
                dve.wait_ge(s_meta, first_tile + (L + 1))
                dve.tensor_copy(meta_tile[:], meta_next[:]).then_inc(s_moved, 1)
                ended = experts(dve, L, tile)
                take_y(ended)

            dve.wait_ge(s_fx, 16)
            for k in range(4):
                dve.wait_ge(s_fz[k], 16)
                part = raw[:, k * PIECE:(k + 1) * PIECE]
                dve.tensor_tensor(part, part, z_flat(k), ALU.add).then_inc(s_final, 1)


def kernel(x, adj, L0_gnn_weight, L0_gnn_bias, L0_ffn_norm_w, L0_ffn_w_macro, L0_ffn_w_micro, L0_ffn_w1, L0_ffn_w2):
    import numpy as np
    import concourse.bacc as bacc
    from concourse.bass_utils import run_bass_kernel_spmd

    x, adj, w1, w2 = (np.asarray(a) for a in (x, adj, L0_ffn_w1, L0_ffn_w2))
    N, D = x.shape
    E, F, _ = w1.shape
    t = -(-N // P)
    pad = t * P - N
    w_route = np.concatenate([np.asarray(L0_ffn_w_macro), np.asarray(L0_ffn_w_micro).reshape(E, D)])
    arrays = {
        "x": np.pad(x, ((0, pad), (0, 0))),
        "adj_t": np.pad(adj, ((0, pad), (0, pad))).reshape(t, P, t, P).transpose(0, 3, 2, 1).reshape(t, P, t * P),
        "gnn_w": np.asarray(L0_gnn_weight),
        "gnn_b": np.asarray(L0_gnn_bias),
        "norm_w": np.asarray(L0_ffn_norm_w),
        "w_route": w_route.T.reshape(D // P, P, -1),
        "w1": w1.transpose(0, 2, 1).reshape(E, D // P, P, F),
        "w2": w2.transpose(0, 2, 1).reshape(E, D // P, F // D, P, D).transpose(0, 1, 3, 2, 4).reshape(E, D // P, P, F),
    }
    arrays = {name: np.ascontiguousarray(a) for name, a in arrays.items()}
    nc = bacc.Bacc("TRN2", target_bir_lowering=False, num_devices=1)
    args = [nc.dram_tensor(name, a.shape, mybir.dt.from_np(a.dtype), kind="ExternalInput").ap()
            for name, a in arrays.items()]
    out = nc.dram_tensor("out", (N, D), F32, kind="ExternalOutput").ap()
    adj_ffn_program(nc, *args, out)
    return run_bass_kernel_spmd(nc, [arrays], core_ids=[0]).results[0]["out"]
```

```python
from contextlib import ExitStack

import concourse.bass as bass
from concourse import mybir
from concourse.alu_op_type import AluOpType as ALU

ACT = mybir.ActivationFunctionType
AX = mybir.AxisListType
F32 = mybir.dt.float32
F32R = mybir.dt.float32r
BF16 = mybir.dt.bfloat16
I32 = mybir.dt.int32
U32 = mybir.dt.uint32

P = 128
LN_EPS = 1e-5
RMS_EPS = 1e-6
EPS = 1e-9
LOOPS = 2
HALF = 512


def adj_ffn_program(nc, N, x, adj_t, gnn_w, gnn_b, norm_w, w_route, w1, w2, out):
    D = x.shape[1]
    n_tiles = x.shape[0] // P
    last_rows = N - (n_tiles - 1) * P
    E, _, _, F = w1.shape
    G = w_route.shape[2] - E
    PICK = E // G
    KD = D // P
    KF = F // P
    HALVES = F // HALF
    CHUNKS = 2 * KD
    CW = F
    REGION = (n_tiles + 1) * P
    ROW = D + 1 + E
    GT = 3
    groups = [list(range(a, min(a + GT, n_tiles))) for a in range(0, n_tiles, GT)]
    NQ = len(groups)
    ADJ = n_tiles * P
    SLOTS = 8
    assert (n_tiles - SLOTS) * ROW <= 2 * F
    AHEAD = 2 * GT
    N_LN = 2 * n_tiles

    with ExitStack() as ctx:
        def sb(name, shape, dt):
            return ctx.enter_context(nc.sbuf_tensor(name, shape, dt))

        def psum(name, shape):
            return ctx.enter_context(nc.psum_tensor(name, shape, F32))

        def sem(name):
            return ctx.enter_context(nc.semaphore(name))

        def dram(name, shape):
            return nc.dram_tensor(name, shape, F32, kind="Internal").ap()

        regions = dram("regions", (E * REGION, ROW))
        z_rows = dram("z_rows", (n_tiles * P + P, D))

        weights = sb("weights", [P, 2, 2, CHUNKS * CW], F32R)
        raw = sb("raw", [P, CHUNKS * CW], F32)
        even_area = weights[:, 0, :, :].rearrange("p a b -> p (a b)")
        odd_area = weights[:, 1, :, :].rearrange("p a b -> p (a b)")
        sup = [even_area[:, h * n_tiles * D:(h + 1) * n_tiles * D] for h in range(2)]
        gw0 = 2 * n_tiles * D
        gw = [even_area[:, gw0 + h * KD * D:gw0 + (h + 1) * KD * D] for h in range(2)]
        adj = [[odd_area[:, (2 * b + h) * ADJ:(2 * b + h + 1) * ADJ] for h in range(2)] for b in range(2)]
        adj_raw = [raw[:, b * ADJ:(b + 1) * ADJ] for b in range(2)]
        XR = 4
        x_raw = [raw[:, 2 * ADJ + b * D:2 * ADJ + (b + 1) * D] for b in range(XR)]
        gw_raw = raw[:, 2 * ADJ + XR * D:2 * ADJ + (XR + KD) * D]
        col0 = 2 * ADJ + (XR + KD) * D
        z_buf = [raw[:, CHUNKS * CW - (2 - b) * D:CHUNKS * CW - (1 - b) * D] for b in range(2)]
        LATE = CHUNKS - 2
        raw_rows = raw[:, LATE * CW:]
        diff = raw[:, col0:col0 + P].bitcast(I32)
        tok_i = raw[:, col0 + P:col0 + P + n_tiles + 1].bitcast(I32)
        base_i = raw[:, col0 + 2 * P:col0 + 2 * P + E].bitcast(I32)

        zn = sb("zn", [P, SLOTS, ROW], F32)
        hidden = sb("hidden", [P, F], F32)
        xin = sb("xin", [P, ROW], F32)
        xT = [sb(f"xT_{h}", [P, KD * P], F32R) for h in ("hi", "lo")]
        hT = [sb(f"hT_{h}", [P, KF * P], F32R) for h in ("hi", "lo")]
        y_out = sb("y_out", [P, D], F32)
        y_row = sb("y_row", [P, 1], U32)
        zT = [y_out, sb("zT", [P, KD * P], F32)]
        w_norm = sb("w_norm", [P, D], F32)
        bias = xin[:, 0:D]
        ident = sb("ident", [P, P], F32)
        before = sb("before", [P, P], BF16)
        ones = sb("ones", [P, P], BF16)
        wr = sb("wr", [P, KD, G + E], F32)
        tok = sb("tok", [P, n_tiles + 1], F32)
        base0 = sb("base0", [P, E], F32)
        base = sb("base", [P, E], F32)
        valid = sb("valid", [P, 1], F32)
        lower = sb("lower", [P, G, G], F32)
        eps_ln = sb("eps_ln", [P, 1], F32)
        eps_rms = sb("eps_rms", [P, 1], F32)
        stats = sb("stats", [P, N_LN, 6], F32)
        mv = sb("mv", [P, N_LN, 2], F32)
        std = sb("std", [P, N_LN], F32)
        rstd = sb("rstd", [P, N_LN], F32)
        sumsq = sb("sumsq", [P, LOOPS * n_tiles], F32)
        rms = sb("rms", [P, LOOPS * n_tiles], F32)
        rrms = sb("rrms", [P, LOOPS * n_tiles], F32)
        lg = sb("lg", [P, GT, G + E], F32)
        gt_ = sb("gt", [P, GT, G, G], F32)
        eq_ = sb("eq", [P, GT, G, G], F32)
        rank = sb("rank", [P, GT, G], F32)
        pick = sb("pick", [P, GT, G, PICK], F32)
        chosen = [sb(f"chosen{s}", [P, GT, E], F32) for s in range(2)]
        mask = sb("mask", [P, GT + 1, E], BF16)
        top = sb("top", [P, GT], F32)
        d1 = sb("d1", [P, GT, G], F32)
        ex_in = sb("ex_in", [P, GT, 2 * G], F32)
        ex = sb("ex", [P, GT, 2 * G], F32)
        esum = sb("esum", [P, GT], F32)
        num = sb("num", [P, GT, G], F32)
        warm = sb("warm", [P, 2 * LOOPS], F32)
        den = sb("den", [P, GT], F32)
        lv = sb("lv", [P, GT, G], F32)
        place = sb("place", [P, GT, E], F32)
        placed = [sb(f"placed{s}", [P, GT, E], F32) for s in range(2)]
        slot_f = sb("slot_f", [P, 2, GT], F32)
        slots = [sb(f"slots{q}", [P, 2, GT], U32) for q in range(NQ)]
        meta_next = sb("meta_next", [P, 1 + E], F32)
        meta_tile = sb("meta_tile", [P, 1 + E], F32)
        meta_y = sb("meta_y", [P, 2], F32)
        n_f = sb("n_f", [1, E], F32)
        n_i = sb("n_i", [1, E], I32)
        n_t = sb("n_t", [1, E], I32)
        pre = [sb(f"pre{k}", [1, 4 + E], F32) for k in range(4)]
        tiles_before = sb("tiles_before", [1, 1], F32)
        tile_table = [sb(f"tile_table{L}", [1, E + 1], I32) for L in range(LOOPS)]
        pad_table = [sb(f"pad_table{L}", [1, E], I32) for L in range(LOOPS)]

        h_ps = psum("h_ps", [P, 2, HALF])
        xt_ps = psum("xt_ps", [P, HALF])
        y_ps = psum("y_ps", [P, HALF])
        ht_ps = psum("ht_ps", [P, 2, HALF])
        lg_ps = psum("lg_ps", [P, HALF])
        rk_ps = psum("rk_ps", [P, HALF])
        turn_ps = [xt_ps, y_ps]
        logit_ps = [lg_ps, ht_ps[:, 1, :]]
        rk = rk_ps[:, 0:(GT + 1) * E].rearrange("p (t e) -> p t e", e=E)

        s_gw = [sem(f"gw_loaded{k}") for k in range(KD)]
        s_const = sem("const_loaded")
        s_x = [sem(f"x_loaded{b}") for b in range(XR)]
        s_adj = [sem(f"adj_loaded{b}") for b in range(2)]
        s_res = [sem(f"residual_loaded{b}") for b in range(2)]
        s_sumst = [sem(f"sum_stored{b}") for b in range(2)]
        s_zst = [sem(f"z_stored{b}") for b in range(2)]
        s_zin = [sem(f"z_loaded{i}") for i in range(n_tiles)]
        s_padz = sem("pad_rows_cleared")
        s_pad = sem("pads_filled")
        s_disp = [sem(f"dispatched{q}") for q in range(NQ)]
        s_xin = sem("xin_loaded")
        s_raw = [sem(f"chunk_loaded{c}") for c in range(CHUNKS)]
        s_zadd = sem("y_added_to_z")
        s_sumadd = sem("y_added_to_sum")
        s_yfree = sem("loop_added")
        s_iota = sem("iotas_made")
        s_made = sem("constants_made")
        s_step = sem("vector_steps")
        s_var = sem("variance_made")
        s_std = sem("std_made")
        s_xn = sem("xn_made")
        s_xnT = sem("xn_turned")
        s_xnh = sem("xn_hi_made")
        s_xnl = sem("xn_lo_made")
        s_gwh = sem("gw_hi_made")
        s_gwl = sem("gw_lo_made")
        s_sup = sem("support_summed")
        s_suph = sem("support_hi_made")
        s_supl = sem("support_lo_made")
        s_adjh = sem("adj_hi_made")
        s_adjl = sem("adj_lo_made")
        s_conv = sem("convolution_summed")
        s_x1 = sem("x1_made")
        s_z = sem("z_made")
        s_sum = sem("x1_plus_z_made")
        s_ss = sem("squares_summed")
        s_rms = sem("rms_made")
        s_zn = sem("zn_made")
        s_znT = sem("zn_turned")
        s_zT = sem("zT_copied")
        s_lg = sem("logits_made")
        s_lgt = sem("logits_taken")
        s_exi = sem("exponents_ready")
        s_exo = sem("exponentials_made")
        s_mask = sem("mask_made")
        s_rank = sem("ranks_made")
        s_slot = sem("slots_made")
        s_table = sem("tables_made")
        s_padt = sem("pad_tile_made")
        s_wh = sem("weight_hi_made")
        s_wl = sem("weight_lo_made")
        s_xt = sem("xin_turned")
        s_xh = sem("xT_hi_made")
        s_xl = sem("xT_lo_made")
        s_meta = sem("meta_taken")
        s_my = sem("meta_y_made")
        s_moved = sem("meta_moved")
        s_h = sem("hidden_half_summed")
        s_silu = sem("silu_half_made")
        s_ht = sem("hidden_half_turned")
        s_hh = sem("hT_hi_half_made")
        s_hl = sem("hT_lo_half_made")
        s_y = sem("y_summed")
        s_yt = sem("y_taken")
        s_begun = sem("y_adding")
        s_done = sem("result_complete")
        s_yf = sem("y_out_free")


        def w1_part(par, h, kd, half):
            c0 = kd * CW + half * HALF
            return weights[:, par, h, c0:c0 + HALF]

        def w2_part(par, h, kf):
            c0 = KD * CW + kf * D
            return weights[:, par, h, c0:c0 + D]

        def chunk(h, par, c):
            return weights[:, par, h, c * CW:(c + 1) * CW]

        def raw_chunk(c):
            return raw[:, c * CW:(c + 1) * CW]

        def table_value(eng, L, e):
            cell = tile_table[L][0:1, e:e + 1] if isinstance(e, int) else tile_table[L][0:1, bass.ds(e, 1)]
            least = (e if isinstance(e, int) else 1) + E * L
            return eng.value_load(cell, min_val=least, max_val=4 * n_tiles * LOOPS)

        def experts(eng, L, tile):
            def one(e, par, start, prev):
                end = table_value(eng, L, e + 1)
                tile(start, e, par, True, prev, start)
                with eng.If(end > start + 1):
                    with eng.Fori(start + 1, end) as g:
                        tile(g, e, par, False, True, start)
                with eng.Else():
                    pass
                return end

            start = one(0, 0, table_value(eng, L, 0), False)
            with eng.Fori(1, E - 3, 2) as e:
                second = one(e, 1, table_value(eng, L, e), True)
                one(e + 1, 0, second, True)
            start = table_value(eng, L, E - 3)
            for e in range(E - 3, E):
                start = one(e, e % 2, start, True)
            return start

        def rows_buffer(L, i, c0=0, c1=ROW):
            if i < SLOTS or L == 0:
                return zn[:, i % SLOTS, c0:c1]
            return raw_rows[:, (i - SLOTS) * ROW + c0:(i - SLOTS) * ROW + c1]

        PAD_SLOT = n_tiles % SLOTS

        def wait_dispatched(eng, L, q):
            eng.wait_ge(s_disp[q], 2 * 16 * len(groups[q]) * (L + 1))

        def rows_of(t):
            return last_rows if t == n_tiles - 1 else P

        block = ctx.enter_context(nc.Block())

        @block.sync
        def _(sp):
            def load_x(i):
                if i >= XR:
                    sp.wait_ge(s_xn, i - XR + 1)
                sp.dma_start(x_raw[i % XR], x[i * P:(i + 1) * P, :]).then_inc(s_x[i % XR], 16)

            def load_adj(i):
                if i >= 2:
                    sp.wait_ge(s_adjl, i - 1)
                sp.dma_start(adj_raw[i % 2], adj_t[i]).then_inc(s_adj[i % 2], 16)

            def load_residual(i):
                b = i % 2
                if i < 2:
                    sp.wait_ge(s_xnT, n_tiles)
                else:
                    sp.wait_ge(s_sumst[b], 16 * (i // 2))
                sp.dma_start(hidden[:, b * D:(b + 1) * D], x[i * P:(i + 1) * P, :]).then_inc(s_res[b], 16)

            for i in range(XR):
                load_x(i)
                if i == 1:
                    for k in range(KD):
                        sp.dma_start(gw_raw[:, k * D:(k + 1) * D], gnn_w[k * P:(k + 1) * P, :]).then_inc(s_gw[k], 16)
            load_adj(0)
            load_adj(1)
            sp.dma_start(bias, gnn_b.partition_broadcast(P)).then_inc(s_const, 16)
            sp.dma_start(w_norm[:], norm_w.partition_broadcast(P)).then_inc(s_const, 16)
            sp.dma_start(wr[:], w_route.rearrange("k p n -> p k n")).then_inc(s_const, 16)
            for i in range(XR, n_tiles):
                load_x(i)
            load_residual(0)
            load_residual(1)
            load_adj(2)
            for i in range(n_tiles):
                if i + 3 < n_tiles:
                    load_adj(i + 3)
                sp.wait_ge(s_z, i + 1)
                sp.dma_start(z_rows[i * P:(i + 1) * P, :], z_buf[i % 2]).then_inc(s_zst[i % 2], 16)
                sp.wait_ge(s_sum, i + 1)
                sp.dma_start(out[i * P:(i + 1) * P, :], hidden[:, i % 2 * D:(i % 2 + 1) * D]
                             ).then_inc(s_sumst[i % 2], 16)
                if i + 2 < n_tiles:
                    load_residual(i + 2)

            for L in range(LOOPS):
                if L > 0:
                    sp.wait_ge(s_zadd, ended * 16)
                    for i in range(n_tiles):
                        if i == SLOTS:
                            sp.wait_ge(s_wl, (E * L + 1) * CHUNKS)
                        sp.dma_start(rows_buffer(L, i, 0, D), z_rows[i * P:(i + 1) * P, :]
                                     ).then_inc(s_zin[i], 16)
                        if i == 0:
                            sp.wait_ge(s_sumadd, ended * 16)
                            sp.nop().then_inc(s_yfree, 1)
                sp.wait_ge(s_padt, L + 1)
                if L == 0:
                    for rows in (z_rows, out):
                        sp.dma_start(rows[n_tiles * P:, :], zn[:, PAD_SLOT, 0:D]).then_inc(s_padz, 16)

                def fill_pads(e):
                    cell = pad_table[L][0:1, e:e + 1] if isinstance(e, int) else pad_table[L][0:1, bass.ds(e, 1)]
                    first_pad = sp.value_load(cell, min_val=0, max_val=(E - 1) * REGION + N)
                    sp.dma_start(regions[bass.ds(first_pad, P), :], zn[:, PAD_SLOT, :]).then_inc(s_pad, 16)

                sp.wait_ge(s_table, L + 1)
                fill_pads(0)

                def load_tile(g, e, par, first, prev, start):
                    if prev or L > 0:
                        sp.wait_ge(s_xt, g + L)
                        sp.wait_ge(s_meta, g + L)
                    if first and isinstance(e, int) and e == 0:
                        sp.wait_ge(s_padz, 32)
                        for q in range(NQ):
                            wait_dispatched(sp, L, q)
                    if first:
                        sp.wait_ge(s_pad, e * 16 + 16 * (E * L + 1))
                    row = e * REGION if first else e * REGION + (g - start) * P
                    if not isinstance(row, int):
                        row = nc.s_assert_within(row, 0, (E - 1) * REGION + ADJ, skip_runtime_bounds_check_because=
                                                 "g is one of the expert's tiles, of which there are at most n_tiles")
                    src = regions[row:row + P, :] if isinstance(row, int) else regions[bass.ds(row, P), :]
                    sp.dma_start(xin[:], src).then_inc(s_xin, 16)
                    if first and not (isinstance(e, int) and e == E - 1):
                        fill_pads(e + 1)

                ended = experts(sp, L, load_tile)
                load_tile(ended, E - 1, 1, True, True, ended)

            for b in range(2):
                sp.wait_ge(s_zst[b], 16 * ((n_tiles + 1 - b) // 2))
                sp.wait_ge(s_sumst[b], 16 * ((n_tiles + 1 - b) // 2))
            sp.wait_ge(s_sumadd, ended * 16)
            sp.nop().then_inc(s_done, 1)

        @block.gpsimd
        def _(pool):
            pool.iota(diff, [[1, P]], base=0, channel_multiplier=-1)
            pool.iota(tok_i, [[P, n_tiles + 1]], base=0, channel_multiplier=1)
            pool.iota(base_i, [[REGION, E]], base=0, channel_multiplier=0).then_inc(s_iota, 1)
            for L in range(LOOPS):
                for q, tiles in enumerate(groups):
                    pool.wait_ge(s_slot, NQ * L + q + 1)
                    for t, i in enumerate(tiles):
                        n = rows_of(i)
                        for s in range(2):
                            pool.indirect_dma_start(
                                regions, bass.IndirectOffsetOnAxis(ap=slots[q][0:n, s, t:t + 1], axis=0),
                                rows_buffer(L, i)[0:n, :], None).then_inc(s_disp[q], 16)
                if L == 0:
                    pool.wait_ge(s_padz, 32)
                    for b in range(2):
                        pool.wait_ge(s_zst[b], 16 * ((n_tiles + 1 - b) // 2))
                        pool.wait_ge(s_sumst[b], 16 * ((n_tiles + 1 - b) // 2))
                pool.wait_ge(s_table, L + 1)
                first_tile = table_value(pool, L, 0)
                ended = table_value(pool, L, E)
                last = L + 1 == LOOPS
                with pool.Fori(first_tile, ended) as g:
                    pool.wait_ge(s_yt, g + 2)
                    pool.sem_inc(s_begun)
                    for rows, added in [(out, s_sumadd)] if last else [(z_rows, s_zadd), (out, s_sumadd)]:
                        pool.indirect_dma_start(
                            rows, bass.IndirectOffsetOnAxis(ap=y_row[:, 0:1], axis=0),
                            y_out[:], None, compute_op=ALU.add).then_inc(added, 16)
                    if not last:
                        pool.wait_ge(s_zadd, g * 16 + 16)
                    pool.wait_ge(s_sumadd, g * 16 + 16)
                    pool.nop().then_inc(s_yf, 1)

        @block.scalar
        def _(act):
            def split_hi(dst, src, ready):
                act.copy(dst, src).then_inc(ready, 1)

            def std_of(i):
                act.wait_ge(s_var, i + 1)
                act.activation(std[:, i:i + 1], mv[:, i, 1:2], ACT.Sqrt, bias=eps_ln[:, 0:1]).then_inc(s_std, 1)

            def adj_hi(i):
                act.wait_ge(s_adj[i % 2], 16 * (i // 2 + 1))
                if i >= 2:
                    act.wait_ge(s_conv, i - 1)
                split_hi(adj[i % 2][0], adj_raw[i % 2], s_adjh)

            def square(n, src):
                if n >= 1:
                    act.wait_ge(s_ss, n)
                act.activation(ht_ps[:, 0, :], src, ACT.Square, accum_out=sumsq[:, n:n + 1]).then_inc(s_ss, 1)

            def root(n, count):
                act.wait_ge(s_ss, n + count)
                act.activation(rms[:, n:n + count], sumsq[:, n:n + count], ACT.Sqrt, scale=1.0 / D,
                               bias=eps_rms[:, 0:1]).then_inc(s_rms, count)

            def copy_zT(n):
                act.wait_ge(s_znT, n + 1)
                if n >= 2:
                    act.wait_ge(s_lg, n - 1)
                act.copy(zT[n % 2][:], turn_ps[n % 2][:]).then_inc(s_zT, 1)

            def exps(Q, nt):
                act.wait_ge(s_exi, Q + 1)
                act.activation(ex[:, 0:nt, :], ex_in[:, 0:nt, :], ACT.Exp).then_inc(s_exo, 1)

            def ready(func, k):
                act.activation(warm[:, k:k + 1], eps_rms[:, 0:1], func)

            def load_chunk(en, c):
                w, k = (w1, c) if c < KD else (w2, c - KD)
                src = w[en, k] if isinstance(en, int) else w[bass.ds(en, 1), k, :, :].rearrange("a p n -> p (a n)")
                act.dma_start(raw_chunk(c), src).then_inc(s_raw[c], 16)

            act.wait_ge(s_made, 1)
            std_of(0)
            std_of(1)
            for k in range(KD):
                act.wait_ge(s_gw[k], 16)
                split_hi(gw[0][:, k * D:(k + 1) * D], gw_raw[:, k * D:(k + 1) * D], s_gwh)
            for i in range(n_tiles + 1):
                if 1 <= i and i + 1 < n_tiles:
                    std_of(i + 1)
                if i >= 1:
                    j = i - 1
                    act.wait_ge(s_xnT, j + 1)
                    if j >= 2:
                        act.wait_ge(s_sup, j - 1)
                    split_hi(hT[0][:, j % 2 * D:(j % 2 + 1) * D], turn_ps[j % 2][:], s_xnh)
                    if j >= 1:
                        act.wait_ge(s_sup, j)
                        split_hi(sup[0][:, (j - 1) * D:j * D], h_ps[:, (j - 1) % 2, :], s_suph)
                if i in (3, 6):
                    adj_hi(i // 3 - 1)
            act.wait_ge(s_sup, n_tiles)
            split_hi(sup[0][:, (n_tiles - 1) * D:], h_ps[:, (n_tiles - 1) % 2, :], s_suph)

            for i in range(n_tiles + 4):
                if i + 2 < n_tiles:
                    adj_hi(i + 2)
                if i < n_tiles:
                    std_of(n_tiles + i)
                if 1 <= i < n_tiles + 1:
                    copy_zT(i - 1)
                if i < n_tiles:
                    act.wait_ge(s_z, i + 1)
                    square(i, z_buf[i % 2])
                    root(i, 1)
                if i == n_tiles - 2:
                    act.wait_ge(s_adjl, n_tiles)
                    for c in range(CHUNKS - 1):
                        load_chunk(0, c)
                for q, tiles in enumerate(groups):
                    if i == tiles[-1] + 2:
                        exps(q, len(tiles))

            act.wait_ge(s_conv, n_tiles)
            for c in range(CHUNKS):
                if c == KD:
                    act.wait_ge(s_sum, n_tiles)
                    for b in range(2):
                        act.wait_ge(s_zst[b], 16 * ((n_tiles + 1 - b) // 2))
                    load_chunk(0, CHUNKS - 1)
                act.wait_ge(s_raw[c], 16)
                split_hi(chunk(0, 0, c), raw_chunk(c), s_wh)
            for c in range(2):
                act.wait_ge(s_wl, c + 1)
                load_chunk(1, c)

            for L in range(LOOPS):
                if L > 0:
                    n0 = n_tiles * L
                    ready(ACT.Sqrt, 2 * L - 2)
                    for q, tiles in enumerate(groups):
                        for i in tiles:
                            act.wait_ge(s_zin[i], 16 * L)
                            square(n0 + i, rows_buffer(L, i, 0, D))
                            if i == AHEAD:
                                act.wait_ge(s_yfree, L)
                            if i >= AHEAD:
                                copy_zT(n0 + i - AHEAD)
                        root(n0 + tiles[0], len(tiles))
                    waiting = list(range(NQ))
                    ready(ACT.Exp, 2 * L - 1)
                    for i in range(n_tiles - AHEAD, n_tiles):
                        while groups[waiting[0]][-1] + 3 <= i:
                            q = waiting.pop(0)
                            exps(NQ * L + q, len(groups[q]))
                        copy_zT(n0 + i)
                    for q in waiting:
                        exps(NQ * L + q, len(groups[q]))

                act.wait_ge(s_table, L + 1)

                def x_hi(g):
                    act.wait_ge(s_xt, g + (L + 1))
                    split_hi(xT[0][:], xt_ps[:], s_xh)

                def tile(g, e, par, first, prev, start):
                    more = first and not (L == LOOPS - 1 and isinstance(e, int) and e == E - 1)
                    load = first and not (L == LOOPS - 1 and isinstance(e, int) and e >= E - 2)
                    en = e + E * L

                    def next_hi(c):
                        act.wait_ge(s_raw[c], 16 * (en + 2) if isinstance(en, int) else en * 16 + 32)
                        if prev or L > 0:
                            if c < KD:
                                act.wait_ge(s_h, start * HALVES)
                            else:
                                act.wait_ge(s_y, start)
                        split_hi(chunk(0, 1 - par, c), raw_chunk(c), s_wh)

                    if more:
                        next_hi(0)
                        next_hi(1)
                    for half in range(HALVES):
                        act.wait_ge(s_h, g * HALVES + (half + 1))
                        act.activation(hidden[:, half * HALF:(half + 1) * HALF], h_ps[:, half, :],
                                       ACT.Silu).then_inc(s_silu, 1)
                        if more and half == 0:
                            next_hi(2)
                    x_hi(g + 1)
                    if more:
                        next_hi(3)
                    if load:
                        for c in range(KD):
                            act.wait_ge(s_wl, en * CHUNKS + (CHUNKS + c + 1))
                            load_chunk((e + 2) % E if isinstance(e, int) else e + 2, c)
                    for half in range(HALVES):
                        act.wait_ge(s_ht, g * HALVES + (half + 1))
                        split_hi(hT[0][:, half * HALF:(half + 1) * HALF], ht_ps[:, half, :], s_hh)
                    if more:
                        for c in range(KD, CHUNKS):
                            next_hi(c)
                    if load:
                        for c in range(KD, LATE if isinstance(e, int) and e == E - 1 else CHUNKS):
                            act.wait_ge(s_wl, en * CHUNKS + (CHUNKS + c + 1))
                            load_chunk((e + 2) % E if isinstance(e, int) else e + 2, c)

                if L == 0:
                    for b in range(2):
                        act.wait_ge(s_sumst[b], 16 * ((n_tiles + 1 - b) // 2))
                ready(ACT.Silu, 2 * LOOPS - 2 + L)
                x_hi(table_value(act, L, 0))
                if L == 0:
                    for c in range(2, CHUNKS):
                        act.wait_ge(s_wl, c + 1)
                        load_chunk(1, c)
                else:
                    for q in range(SLOTS // GT, NQ):
                        wait_dispatched(act, L, q)
                    for c in range(LATE, CHUNKS):
                        load_chunk(1, c)
                experts(act, L, tile)

        @block.tensor
        def _(pe):
            def turn(dst, src, kd0, n, ready):
                for k in range(n):
                    m = pe.transpose(dst[:, k * P:(k + 1) * P], src[:, (kd0 + k) * P:(kd0 + k + 1) * P], ident[:])
                m.then_inc(ready, 1)

            def product(dst, pairs, ready):
                for k, ((ah, al), (bh, bl)) in enumerate(pairs):
                    pe.matmul(dst, ah, bh, start=(k == 0), stop=False)
                    pe.matmul(dst, ah, bl, start=False, stop=False)
                    m = pe.matmul(dst, al, bh, start=False, stop=(k == len(pairs) - 1))
                m.then_inc(ready, 1)

            def turn_zn(n):
                L, i = divmod(n, n_tiles)
                pe.wait_ge(s_zn, n + 1)
                if n >= 2:
                    pe.wait_ge(s_zT, n - 1)
                turn(turn_ps[n % 2], rows_buffer(L, i), 0, KD, s_znT)

            def logits(n, Q, t):
                pe.wait_ge(s_zT, n + 1)
                if t == 0 and Q > 1:
                    pe.wait_ge(s_lgt, Q - 1)
                c0 = t * (G + E)
                for k in range(KD):
                    m = pe.matmul(logit_ps[Q % 2][:, c0:c0 + G + E], zT[n % 2][:, k * P:(k + 1) * P], wr[:, k, :],
                                  start=(k == 0), stop=(k == KD - 1))
                m.then_inc(s_lg, 1)

            def ranks(Q, nt):
                pe.wait_ge(s_mask, Q + 1)
                pe.matmul(rk_ps[:, 0:(nt + 1) * E], before[:], mask[:, 0:nt + 1, :].rearrange("p t e -> p (t e)"),
                          start=True, stop=True)
                for t in range(nt):
                    m = pe.matmul(rk[:, t + 1:nt + 1, :], ones[:],
                                  mask[:, t:t + 1, :].broadcast_to([P, nt - t, E]),
                                  start=False, stop=True, skip_group_check=True)
                m.then_inc(s_rank, 1)

            pe.wait_ge(s_made, 1)
            for i in range(n_tiles + 1):
                if i < n_tiles:
                    pe.wait_ge(s_xn, i + 1)
                    if i >= 2:
                        pe.wait_ge(s_xnl, i - 1)
                    turn(turn_ps[i % 2], hidden[:, i % 2 * D:(i % 2 + 1) * D], 0, KD, s_xnT)
                if i >= 1:
                    j = i - 1
                    if j == 0:
                        pe.wait_ge(s_gwl, KD)
                    pe.wait_ge(s_xnl, j + 1)
                    if j >= 2:
                        pe.wait_ge(s_supl, j - 1)
                    c0 = j % 2 * D
                    product(h_ps[:, j % 2, :],
                            [([hT[h][:, c0 + k * P:c0 + (k + 1) * P] for h in range(2)],
                              [gw[h][:, k * D:(k + 1) * D] for h in range(2)]) for k in range(KD)], s_sup)
            pe.wait_ge(s_supl, n_tiles)
            for i in range(n_tiles + 4):
                if i < n_tiles:
                    pe.wait_ge(s_adjl, i + 1)
                    if i >= 2:
                        pe.wait_ge(s_x1, i - 1)
                    product(h_ps[:, i % 2, :],
                            [([adj[i % 2][h][:, j * P:(j + 1) * P] for h in range(2)],
                              [sup[h][:, j * D:(j + 1) * D] for h in range(2)]) for j in range(n_tiles)], s_conv)
                if 2 <= i < n_tiles + 2:
                    logits(i - 2, (i - 2) // GT, (i - 2) % GT)
                if 1 <= i < n_tiles + 1:
                    turn_zn(i - 1)
                for q, tiles in enumerate(groups):
                    if i == tiles[-1] + 3:
                        ranks(q, len(tiles))

            for L in range(LOOPS):
                if L > 0:
                    for i in range(n_tiles + 4):
                        n = n_tiles * L + i
                        if i < n_tiles:
                            turn_zn(n)
                        if 1 <= i < n_tiles + 1:
                            logits(n - 1, NQ * L + (i - 1) // GT, (i - 1) % GT)
                        for q, tiles in enumerate(groups):
                            if i == tiles[-1] + 2:
                                ranks(NQ * L + q, len(tiles))
                pe.wait_ge(s_table, L + 1)

                def turn_x(g):
                    pe.wait_ge(s_xin, g * 16 + 16 * (L + 1))
                    turn(xt_ps, xin, 0, KD, s_xt)

                def y_product(nxt, par, chunks):
                    pe.wait_ge(s_wl, chunks)
                    pe.wait_ge(s_yt, nxt)
                    for half in range(HALVES):
                        pe.wait_ge(s_hl, nxt * HALVES + (half + 1))
                        for kf in range(half * KF // HALVES, (half + 1) * KF // HALVES):
                            ah, al = (hT[h][:, kf * P:(kf + 1) * P] for h in range(2))
                            pe.matmul(y_ps[:], ah, w2_part(par, 0, kf), start=(kf == 0), stop=False)
                            pe.matmul(y_ps[:], ah, w2_part(par, 1, kf), start=False, stop=False)
                            m = pe.matmul(y_ps[:], al, w2_part(par, 0, kf), start=False, stop=(kf == KF - 1))
                    m.then_inc(s_y, 1)

                def tile(g, e, par, first, prev, start):
                    en = e + E * L
                    if first:
                        pe.wait_ge(s_wl, en * CHUNKS + KD)
                    pe.wait_ge(s_xl, g + (L + 1))
                    for half in range(HALVES):
                        product(h_ps[:, half, :],
                                [([xT[h][:, k * P:(k + 1) * P] for h in range(2)],
                                  [w1_part(par, h, k, half) for h in range(2)]) for k in range(KD)], s_h)
                    turn_x(g + 1)
                    if prev:
                        y_product(g, 1 - par if first else par, en * CHUNKS + (0 if first else CHUNKS))
                    for half in range(HALVES):
                        pe.wait_ge(s_silu, g * HALVES + (half + 1))
                        turn(ht_ps[:, half, :], hidden, half * KD, KD, s_ht)

                turn_x(table_value(pe, L, 0))
                ended = experts(pe, L, tile)
                y_product(ended, (E - 1) % 2, E * (L + 1) * CHUNKS)

        @block.vector
        def _(dve):
            steps = [0]

            def step(ins):
                steps[0] += 1
                ins.then_inc(s_step, 1)
                dve.wait_ge(s_step, steps[0])

            def lo(dst, src, hi, ready):
                dve.tensor_tensor(dst, src, hi.bitcast(F32), ALU.subtract).then_inc(ready, 1)

            def moments(i, src):
                step(dve.bn_stats(stats[:, i, :], src))
                dve.bn_aggr(mv[:, i, :], stats[:, i, :]).then_inc(s_var, 1)

            def normalise(i, dst, src, ready):
                dve.wait_ge(s_std, i + 1)
                step(dve.reciprocal(rstd[:, i:i + 1], std[:, i:i + 1]))
                dve.tensor_scalar(dst, src, mv[:, i, 0:1], rstd[:, i:i + 1], ALU.subtract,
                                  ALU.mult).then_inc(ready, 1)

            def adj_lo(i):
                dve.wait_ge(s_adjh, i + 1)
                lo(adj[i % 2][1], adj_raw[i % 2], adj[i % 2][0], s_adjl)

            def make_zn(n, dst, src):
                dve.scalar_tensor_tensor(out=dst, in0=src, scalar=rrms[:, n:n + 1], in1=w_norm[:], op0=ALU.mult,
                                         op1=ALU.mult).then_inc(s_zn, 1)

            def rrms_of(n, count):
                dve.wait_ge(s_rms, n + count)
                step(dve.reciprocal(rrms[:, n:n + count], rms[:, n:n + count]))

            def bc(ap, shape):
                return ap.broadcast_to(shape)

            def route_a(Q, tiles):
                nt = len(tiles)
                t_ = slice(0, nt)
                flat_g = lambda a: a[:, t_, :, :].rearrange("p t g k -> p t (g k)")
                dve.wait_ge(s_lg, n_tiles * (Q // NQ) + tiles[-1] + 1)
                dve.tensor_copy(lg[:, t_, :].rearrange("p t e -> p (t e)"), logit_ps[Q % 2][:, 0:nt * (G + E)]
                                ).then_inc(s_lgt, 1)
                dve.wait_ge(s_lgt, Q + 1)
                macro = lg[:, t_, 0:G]
                u = lg[:, t_, G:].rearrange("p t (g k) -> p t g k", k=PICK)
                other = bc(macro.unsqueeze(2), [P, nt, G, G])
                own = bc(macro.unsqueeze(3), [P, nt, G, G])
                low = bc(lower[:].rearrange("p g k -> p (g k)").unsqueeze(1), [P, nt, G * G])
                dve.tensor_reduce(top[:, t_], macro, AX.X, ALU.max)
                dve.tensor_tensor(d1[:, t_, :], u[:, :, :, 0], u[:, :, :, 1], ALU.subtract)
                dve.tensor_tensor(pick[:, t_, :, 0], u[:, :, :, 0], u[:, :, :, 1], ALU.is_ge)
                dve.tensor_tensor(pick[:, t_, :, 1], u[:, :, :, 0], u[:, :, :, 1], ALU.is_lt)
                dve.tensor_tensor(gt_[:, t_, :, :], other, own, ALU.is_gt)
                step(dve.tensor_tensor(eq_[:, t_, :, :], other, own, ALU.is_equal))
                dve.tensor_tensor(ex_in[:, t_, 0:G], macro, bc(top[:, t_].unsqueeze(2), [P, nt, G]), ALU.subtract)
                dve.scalar_tensor_tensor(out=ex_in[:, t_, G:], in0=d1[:, t_, :], scalar=-1.0, in1=d1[:, t_, :],
                                         op0=ALU.mult, op1=ALU.min).then_inc(s_exi, 1)
                step(dve.tensor_tensor(flat_g(eq_), flat_g(eq_), low, ALU.mult))
                step(dve.tensor_tensor(flat_g(gt_), flat_g(gt_), flat_g(eq_), ALU.add))
                step(dve.tensor_reduce(rank[:, t_, :], gt_[:, t_, :, :], AX.X, ALU.add))
                for s in range(2):
                    ins = dve.scalar_tensor_tensor(
                        out=chosen[s][:, t_, :].rearrange("p t (g k) -> p (t g) k", k=PICK),
                        in0=bc(rank[:, t_, :].rearrange("p t g -> p (t g)").unsqueeze(2), [P, nt * G, PICK]),
                        scalar=float(s), in1=pick[:, t_, :, :].rearrange("p t g k -> p (t g) k"),
                        op0=ALU.is_equal, op1=ALU.mult)
                step(ins)
                dve.memset(mask[:, nt, :], 0.0)
                full = nt - 1 if tiles[-1] == n_tiles - 1 else nt
                ins = dve.tensor_tensor(mask[:, 0:full, :], chosen[0][:, 0:full, :], chosen[1][:, 0:full, :], ALU.add)
                if full < nt:
                    step(dve.tensor_tensor(placed[0][:, full, :], chosen[0][:, full, :], chosen[1][:, full, :],
                                           ALU.add))
                    ins = dve.tensor_scalar(mask[:, full, :], placed[0][:, full, :], valid[:, 0:1], None, ALU.mult)
                ins.then_inc(s_mask, 1)

            def route_b(Q, tiles):
                L = Q // NQ
                nt = len(tiles)
                t_ = slice(0, nt)
                dve.wait_ge(s_exo, Q + 1)
                dve.tensor_reduce(esum[:, t_], ex[:, t_, 0:G], AX.X, ALU.add)
                dve.scalar_tensor_tensor(out=num[:, t_, :], in0=rank[:, t_, :], scalar=2.0, in1=ex[:, t_, 0:G],
                                         op0=ALU.is_lt, op1=ALU.mult)
                dve.tensor_scalar(lv[:, t_, :], ex[:, t_, G:], EPS, 1.0 + EPS, ALU.mult, ALU.add)
                dve.wait_ge(s_rank, Q + 1)
                step(dve.tensor_tensor(place[:, t_, :], rk[:, t_, :], bc(base[:].unsqueeze(1), [P, nt, E]), ALU.add))
                dve.tensor_reduce(den[:, t_], num[:, t_, :], AX.X, ALU.add)
                dve.reciprocal(lv[:, t_, :], lv[:, t_, :])
                dve.tensor_tensor(base[:], base[:], rk[:, nt, :], ALU.add)
                for s in range(2):
                    ins = dve.tensor_tensor(placed[s][:, t_, :], place[:, t_, :], chosen[s][:, t_, :], ALU.mult)
                step(ins)
                dve.scalar_tensor_tensor(out=den[:, t_], in0=esum[:, t_], scalar=EPS, in1=den[:, t_],
                                         op0=ALU.mult, op1=ALU.add)
                dve.tensor_tensor(num[:, t_, :], num[:, t_, :], lv[:, t_, :], ALU.mult)
                for s in range(2):
                    ins = dve.tensor_reduce(slot_f[:, s, t_], placed[s][:, t_, :], AX.X, ALU.add)
                step(ins)
                step(dve.reciprocal(den[:, t_], den[:, t_]))
                dve.tensor_copy(slots[Q % NQ][:, :, t_], slot_f[:, :, t_])
                for i in tiles:
                    dve.tensor_copy(rows_buffer(L, i, D, D + 1), tok[:, i:i + 1])
                step(dve.tensor_tensor(num[:, t_, :], num[:, t_, :], bc(den[:, t_].unsqueeze(2), [P, nt, G]),
                                       ALU.mult))
                for t, i in enumerate(tiles):
                    ins = dve.tensor_tensor(rows_buffer(L, i, D + 1).rearrange("p (g k) -> p g k", k=PICK),
                                            bc(num[:, t, :].unsqueeze(2), [P, G, PICK]), pick[:, t, :, :], ALU.mult)
                ins.then_inc(s_slot, 1)

            def tables(L):
                step(dve.tensor_copy(pad_table[L][:], base[0:1, :]))
                step(dve.tensor_tensor(n_f[:], base[0:1, :], base0[0:1, :], ALU.subtract))
                step(dve.tensor_scalar(n_i[:], n_f[:], float(P - 1), None, ALU.add))
                step(dve.tensor_scalar(n_t[:], n_i[:], P.bit_length() - 1, None, ALU.logical_shift_right))
                step(dve.tensor_scalar(pre[0][:, 4:], n_t[:], 1.0, None, ALU.max))
                for k in range(3):
                    step(dve.tensor_tensor(pre[k + 1][:, 4:], pre[k][:, 4:], pre[k][:, 4 - 2 ** k:4 + E - 2 ** k],
                                           ALU.add))
                dve.tensor_copy(tile_table[L][:, 0:1], tiles_before[:])
                step(dve.tensor_scalar(tile_table[L][:, 1:], pre[3][:, 4:], tiles_before[:, 0:1], None, ALU.add))
                dve.tensor_tensor(tiles_before[:], tiles_before[:], pre[3][:, 3 + E:], ALU.add).then_inc(s_table, 1)

            def pad_tile(L):
                wait_dispatched(dve, L, PAD_SLOT // GT)
                step(dve.memset(zn[:, PAD_SLOT, :], 0.0))
                dve.tensor_copy(zn[:, PAD_SLOT, D:D + 1], tok[:, n_tiles:n_tiles + 1]).then_inc(s_padt, 1)

            dve.memset(ones[:], 1.0)
            dve.memset(eps_ln[:], LN_EPS)
            dve.memset(eps_rms[:], RMS_EPS)
            for k in range(4):
                dve.memset(pre[k][:, 0:4], 0.0)
            dve.memset(tiles_before[:], 0.0)
            dve.memset(lower[:], 0.0)
            step(dve.memset(valid[:], 0.0))
            for g in range(1, G):
                dve.memset(lower[:, g, 0:g], 1.0)
            dve.memset(valid[0:last_rows, :], 1.0)
            dve.wait_ge(s_iota, 1)
            dve.tensor_scalar(ident[:], diff, 0.0, None, ALU.is_equal)
            dve.tensor_scalar(before[:], diff, 0.0, None, ALU.is_gt)
            dve.tensor_copy(tok[:], tok_i)
            dve.tensor_copy(base0[:], base_i)
            dve.tensor_copy(base[:], base_i).then_inc(s_made, 1)
            dve.nop().then_inc(s_yt, 1)
            dve.nop().then_inc(s_yf, 1)
            dve.nop().then_inc(s_hl, HALVES)

            def sup_lo(j):
                c = slice(j * D, (j + 1) * D)
                dve.wait_ge(s_suph, j + 1)
                lo(sup[1][:, c], h_ps[:, j % 2, :], sup[0][:, c], s_supl)

            for i in range(n_tiles + 1):
                if i >= 3:
                    sup_lo(i - 3)
                for j in range(i if i == 0 else i + 1, min(i + 2, n_tiles)):
                    dve.wait_ge(s_x[j % XR], 16 * (j // XR + 1))
                    moments(j, x_raw[j % XR])
                if i < n_tiles:
                    if i >= 2:
                        dve.wait_ge(s_xnT, i - 1)
                    normalise(i, hidden[:, i % 2 * D:(i % 2 + 1) * D], x_raw[i % XR], s_xn)
                if i == 0:
                    for k in range(KD):
                        c = slice(k * D, (k + 1) * D)
                        dve.wait_ge(s_gwh, k + 1)
                        lo(gw[1][:, c], gw_raw[:, c], gw[0][:, c], s_gwl)
                if i >= 1:
                    j = i - 1
                    c = slice(j % 2 * D, (j % 2 + 1) * D)
                    dve.wait_ge(s_xnh, j + 1)
                    lo(hT[1][:, c], turn_ps[j % 2][:], hT[0][:, c], s_xnl)
                if i in (4, 7):
                    adj_lo(i // 3 - 1)
            for j in (n_tiles - 2, n_tiles - 1):
                sup_lo(j)

            dve.wait_ge(s_const, 48)
            for i in range(n_tiles + 4):
                if i < n_tiles:
                    half = hidden[:, i % 2 * D:(i % 2 + 1) * D]
                    z = z_buf[i % 2]
                    dve.wait_ge(s_conv, i + 1)
                    dve.wait_ge(s_res[i % 2], 16 * (i // 2 + 1))
                    step(dve.tensor_tensor(half, h_ps[:, i % 2, :], half, ALU.add))
                    dve.tensor_tensor(half, half, bias, ALU.add).then_inc(s_x1, 1)
                    dve.wait_ge(s_x1, i + 1)
                    moments(n_tiles + i, half)
                    if i + 2 < n_tiles:
                        adj_lo(i + 2)
                    if i >= 2:
                        dve.wait_ge(s_zst[i % 2], 16 * (i // 2))
                    normalise(n_tiles + i, z, half, s_z)
                for q, tiles in enumerate(groups):
                    if i == tiles[-1] + 2:
                        route_a(q, tiles)
                if i < n_tiles:
                    dve.wait_ge(s_z, i + 1)
                    rrms_of(i, 1)
                    if i >= SLOTS:
                        wait_dispatched(dve, 0, (i - SLOTS) // GT)
                    make_zn(i, rows_buffer(0, i, 0, D), z)
                    dve.tensor_tensor(half, half, z, ALU.add).then_inc(s_sum, 1)
                for q, tiles in enumerate(groups):
                    if i == tiles[-1] + 3:
                        route_b(q, tiles)

            def weight_lo(par, c, en):
                dve.wait_ge(s_wh, en * CHUNKS + (c + 1))
                lo(chunk(1, par, c), raw_chunk(c), chunk(0, par, c), s_wl)

            for L in range(LOOPS):
                if L > 0:
                    step(dve.tensor_copy(base[:], base0[:]))
                    for q in range(NQ + 2):
                        if q < NQ:
                            n = n_tiles * L + groups[q][0]
                            rrms_of(n, len(groups[q]))
                            for i in groups[q]:
                                make_zn(n_tiles * L + i, rows_buffer(L, i, 0, D), rows_buffer(L, i, 0, D))
                        if q >= 2:
                            route_b(NQ * L + q - 2, groups[q - 2])
                        if 1 <= q <= NQ:
                            route_a(NQ * L + q - 1, groups[q - 1])
                tables(L)
                dve.wait_ge(s_table, L + 1)
                pad_tile(L)
                if L == 0:
                    for c in range(CHUNKS):
                        weight_lo(0, c, 0)

                def x_lo(g):
                    dve.wait_ge(s_xh, g + (L + 1))
                    lo(xT[1][:], xt_ps[:], xT[0][:], s_xl)
                    if L > 0 or g is not first_tile:
                        dve.wait_ge(s_moved, g + L)
                    dve.tensor_copy(meta_next[:], xin[:, D:]).then_inc(s_meta, 1)

                def take_y(nxt):
                    dve.wait_ge(s_y, nxt)
                    dve.wait_ge(s_yf, nxt)
                    dve.tensor_copy(y_row[:], meta_y[:, 0:1])
                    dve.tensor_scalar(y_out[:], y_ps[:], meta_y[:, 1:2], None, ALU.mult).then_inc(s_yt, 1)

                def tile(g, e, par, first, prev, start):
                    more = first and not (L == LOOPS - 1 and isinstance(e, int) and e == E - 1)
                    en = e + E * L + 1
                    if more:
                        for c in range(3):
                            weight_lo(1 - par, c, en)
                    x_lo(g + 1)
                    if more:
                        weight_lo(1 - par, 3, en)
                    if prev:
                        take_y(g)
                    dve.wait_ge(s_yt, g + 1)
                    dve.wait_ge(s_moved, g + (L + 1))
                    dve.tensor_copy(meta_y[:, 0:1], meta_tile[:, 0:1])
                    w_col = meta_tile[:, 1 + e:2 + e] if isinstance(e, int) else meta_tile[:, bass.ds(e + 1, 1)]
                    dve.tensor_copy(meta_y[:, 1:2], w_col).then_inc(s_my, 1)
                    dve.wait_ge(s_my, g + 1)
                    dve.wait_ge(s_meta, g + (L + 2))
                    dve.tensor_copy(meta_tile[:], meta_next[:]).then_inc(s_moved, 1)
                    for half in range(HALVES):
                        c = slice(half * HALF, (half + 1) * HALF)
                        dve.wait_ge(s_hh, g * HALVES + (half + 1))
                        lo(hT[1][:, c], ht_ps[:, half, :], hT[0][:, c], s_hl)
                    if more:
                        for c in range(KD, CHUNKS):
                            weight_lo(1 - par, c, en)

                first_tile = table_value(dve, L, 0)
                x_lo(first_tile)
                dve.wait_ge(s_meta, first_tile + (L + 1))
                dve.tensor_copy(meta_tile[:], meta_next[:]).then_inc(s_moved, 1)
                ended = experts(dve, L, tile)
                take_y(ended)



def kernel(x, adj, L0_gnn_weight, L0_gnn_bias, L0_ffn_norm_w, L0_ffn_w_macro, L0_ffn_w_micro, L0_ffn_w1, L0_ffn_w2):
    import numpy as np
    import concourse.bacc as bacc
    from concourse.bass_utils import run_bass_kernel_spmd

    x, adj, w1, w2 = (np.asarray(a) for a in (x, adj, L0_ffn_w1, L0_ffn_w2))
    N, D = x.shape
    E, F, _ = w1.shape
    t = -(-N // P)
    pad = t * P - N
    w_route = np.concatenate([np.asarray(L0_ffn_w_macro), np.asarray(L0_ffn_w_micro).reshape(E, D)])
    arrays = {
        "x": np.pad(x, ((0, pad), (0, 0))),
        "adj_t": np.pad(adj, ((0, pad), (0, pad))).reshape(t, P, t, P).transpose(0, 3, 2, 1).reshape(t, P, t * P),
        "gnn_w": np.asarray(L0_gnn_weight),
        "gnn_b": np.asarray(L0_gnn_bias),
        "norm_w": np.asarray(L0_ffn_norm_w),
        "w_route": w_route.T.reshape(D // P, P, -1),
        "w1": w1.transpose(0, 2, 1).reshape(E, D // P, P, F),
        "w2": w2.transpose(0, 2, 1).reshape(E, D // P, F // D, P, D).transpose(0, 1, 3, 2, 4).reshape(E, D // P, P, F),
    }
    arrays = {name: np.ascontiguousarray(a) for name, a in arrays.items()}
    nc = bacc.Bacc("TRN2", target_bir_lowering=False, num_devices=1)
    args = [nc.dram_tensor(name, a.shape, mybir.dt.from_np(a.dtype), kind="ExternalInput").ap()
            for name, a in arrays.items()]
    out = nc.dram_tensor("out", ((t + 1) * P, D), F32, kind="ExternalOutput").ap()
    adj_ffn_program(nc, N, *args, out)
    return run_bass_kernel_spmd(nc, [arrays], core_ids=[0]).results[0]["out"][:N]
```
